# Optimizing a Trainium2 kernel written in Bass

```python
import numpy as np
import jax
import jax.numpy as jnp

def _softmax(x, axis=-1):
    return jax.nn.softmax(x, axis=axis)

def _gelu(x):
    return jax.nn.gelu(x, approximate=True)

def _silu(x):
    return jax.nn.silu(x)

def _sigmoid(x):
    return jax.nn.sigmoid(x)

def _layernorm(x, axis=-1, eps=1e-05):
    m = jnp.mean(x, axis=axis, keepdims=True)
    v = jnp.var(x, axis=axis, keepdims=True)
    return (x - m) / jnp.sqrt(v + eps)

def _scatter_add(tgt, idx, src, axis=0):
    return tgt.at[idx].add(src)

def _segment_sum(src, seg, n):
    return jax.ops.segment_sum(src, seg, n)
kernel_name = 'mk_seq_preln_d1_jaxref_r4_c34ff3'

def setup_inputs(seed: int=0):
    np.random.seed(seed)
    _w = jnp.asarray

    def _L0_attn_setup():
        import jax, jax.numpy as jnp
        import numpy as np
        H, D = (8, 128)
        HID = 256
        K = 4
        EPS_QK = 1e-06
        EPS_NORM = 1e-05

        def short_conv(x, w):
            k = w.shape[-1]
            xp = jnp.pad(x, ((0, 0), (k - 1, 0), (0, 0)))
            xc = jnp.transpose(xp, (0, 2, 1))
            y = jax.lax.conv_general_dilated(xc, w, window_strides=(1,), padding='VALID', feature_group_count=w.shape[0])
            return jax.nn.silu(jnp.transpose(y, (0, 2, 1)))

        def _rmsn(t, eps):
            return t * jax.lax.rsqrt(jnp.mean(t * t, axis=-1, keepdims=True) + eps)
        key = jax.random.key(seed)
        ks = jax.random.split(key, 16)
        s = 0.02
        inp = {'x': jax.random.normal(ks[0], (2, 256, HID), dtype=jnp.float32), 'Wq': jax.random.normal(ks[1], (H * D, HID), dtype=jnp.float32) * s, 'Wk': jax.random.normal(ks[2], (H * D, HID), dtype=jnp.float32) * s, 'Wv': jax.random.normal(ks[3], (H * D, HID), dtype=jnp.float32) * s, 'wq_conv': jax.random.normal(ks[4], (H * D, 1, K), dtype=jnp.float32) * 0.3, 'wk_conv': jax.random.normal(ks[5], (H * D, 1, K), dtype=jnp.float32) * 0.3, 'wv_conv': jax.random.normal(ks[6], (H * D, 1, K), dtype=jnp.float32) * 0.3, 'Wfa': jax.random.normal(ks[7], (D, HID), dtype=jnp.float32) * s, 'Wfb': jax.random.normal(ks[8], (H * D, D), dtype=jnp.float32) * s, 'Wb': jax.random.normal(ks[9], (H, HID), dtype=jnp.float32) * s, 'Wga': jax.random.normal(ks[10], (D, HID), dtype=jnp.float32) * s, 'Wgb': jax.random.normal(ks[11], (H * D, D), dtype=jnp.float32) * s, 'A_log': jnp.log(jax.random.uniform(ks[12], (H,), minval=1.0, maxval=16.0, dtype=jnp.float32)), 'dt_bias': jnp.zeros((H, D), dtype=jnp.float32), 'o_norm_w': jnp.ones((D,), dtype=jnp.float32), 'Wo': jax.random.normal(ks[13], (HID, H * D), dtype=jnp.float32) * s}
        return inp
    _L0_attn_in = _L0_attn_setup()

    def _L0_ffn_setup():
        import jax, jax.numpy as jnp
        import numpy as np
        DIM = 256
        INTER = 128
        E = 8
        TOP_K = 2
        ROUTE_SCALE = 1.0
        key = jax.random.key(seed)
        ks = jax.random.split(key, 8)
        s_d = 1.0 / np.sqrt(DIM)
        s_f = 1.0 / np.sqrt(INTER)
        x = jax.random.normal(ks[0], (2, 512, DIM), dtype=jnp.float32)
        gate_w = jax.random.uniform(ks[1], (E, DIM), jnp.float32, -s_d, s_d)
        wg = jax.random.uniform(ks[2], (E, INTER, DIM), jnp.float32, -s_d, s_d)
        wu = jax.random.uniform(ks[3], (E, INTER, DIM), jnp.float32, -s_d, s_d)
        wd = jax.random.uniform(ks[4], (E, DIM, INTER), jnp.float32, -s_f, s_f)
        sg = jax.random.uniform(ks[5], (INTER, DIM), jnp.float32, -s_d, s_d)
        su = jax.random.uniform(ks[6], (INTER, DIM), jnp.float32, -s_d, s_d)
        sd = jax.random.uniform(ks[7], (DIM, INTER), jnp.float32, -s_f, s_f)
        return {'x': x, 'gate_w': gate_w, 'wg': wg, 'wu': wu, 'wd': wd, 'sg': sg, 'su': su, 'sd': sd}
    _L0_ffn_in = _L0_ffn_setup()
    _d = {'L0_attn_x': _L0_attn_in['x'], 'L0_attn_Wq': _L0_attn_in['Wq'], 'L0_attn_Wk': _L0_attn_in['Wk'], 'L0_attn_Wv': _L0_attn_in['Wv'], 'L0_attn_wq_conv': _L0_attn_in['wq_conv'], 'L0_attn_wk_conv': _L0_attn_in['wk_conv'], 'L0_attn_wv_conv': _L0_attn_in['wv_conv'], 'L0_attn_Wfa': _L0_attn_in['Wfa'], 'L0_attn_Wfb': _L0_attn_in['Wfb'], 'L0_attn_Wb': _L0_attn_in['Wb'], 'L0_attn_Wga': _L0_attn_in['Wga'], 'L0_attn_Wgb': _L0_attn_in['Wgb'], 'L0_attn_A_log': _L0_attn_in['A_log'], 'L0_attn_dt_bias': _L0_attn_in['dt_bias'], 'L0_attn_o_norm_w': _L0_attn_in['o_norm_w'], 'L0_attn_Wo': _L0_attn_in['Wo'], 'L0_ffn_gate_w': _L0_ffn_in['gate_w'], 'L0_ffn_wg': _L0_ffn_in['wg'], 'L0_ffn_wu': _L0_ffn_in['wu'], 'L0_ffn_wd': _L0_ffn_in['wd'], 'L0_ffn_sg': _L0_ffn_in['sg'], 'L0_ffn_su': _L0_ffn_in['su'], 'L0_ffn_sd': _L0_ffn_in['sd']}
    _x0 = _d['L0_attn_x']
    _d['L0_attn_x'] = jax.random.normal(jax.random.fold_in(jax.random.key(seed), 1), (16, 512, 256), dtype=_x0.dtype)
    del _x0
    return _d

def reference(L0_attn_x, L0_attn_Wq, L0_attn_Wk, L0_attn_Wv, L0_attn_wq_conv, L0_attn_wk_conv, L0_attn_wv_conv, L0_attn_Wfa, L0_attn_Wfb, L0_attn_Wb, L0_attn_Wga, L0_attn_Wgb, L0_attn_A_log, L0_attn_dt_bias, L0_attn_o_norm_w, L0_attn_Wo, L0_ffn_gate_w, L0_ffn_wg, L0_ffn_wu, L0_ffn_wd, L0_ffn_sg, L0_ffn_su, L0_ffn_sd):

    def _L0_attn_ref(x, Wq, Wk, Wv, wq_conv, wk_conv, wv_conv, Wfa, Wfb, Wb, Wga, Wgb, A_log, dt_bias, o_norm_w, Wo):
        import jax, jax.numpy as jnp
        import numpy as np
        H, D = (8, 128)
        HID = 256
        K = 4
        EPS_QK = 1e-06
        EPS_NORM = 1e-05

        def short_conv(x, w):
            k = w.shape[-1]
            xp = jnp.pad(x, ((0, 0), (k - 1, 0), (0, 0)))
            xc = jnp.transpose(xp, (0, 2, 1))
            y = jax.lax.conv_general_dilated(xc, w, window_strides=(1,), padding='VALID', feature_group_count=w.shape[0])
            return jax.nn.silu(jnp.transpose(y, (0, 2, 1)))

        def _rmsn(t, eps):
            return t * jax.lax.rsqrt(jnp.mean(t * t, axis=-1, keepdims=True) + eps)
        B, T, _ = x.shape
        scale = float(D) ** (-0.5)
        q = short_conv(x @ Wq.T, wq_conv).reshape(B, T, H, D)
        k = short_conv(x @ Wk.T, wk_conv).reshape(B, T, H, D)
        v = short_conv(x @ Wv.T, wv_conv).reshape(B, T, H, D)
        q = scale ** 2 * _rmsn(q, EPS_QK)
        k = scale * _rmsn(k, EPS_QK)
        a_logits = (x @ Wfa.T @ Wfb.T).reshape(B, T, H, D)
        g = -jnp.exp(A_log)[None, None, :, None] * jax.nn.softplus(a_logits + dt_bias)
        beta = jax.nn.sigmoid(x @ Wb.T)

        def step(S, inputs):
            q_t, k_t, v_t, g_t, b_t = inputs
            S = S * jnp.exp(g_t)[..., None]
            kv = jnp.einsum('bhd,bhdv->bhv', k_t, S)
            delta = b_t[..., None] * (v_t - kv)
            S = S + k_t[..., None] * delta[:, :, None, :]
            o = jnp.einsum('bhd,bhdv->bhv', q_t, S)
            return (S, o)
        tb = lambda t: jnp.moveaxis(t, 1, 0)
        S0 = jnp.zeros((B, H, D, D), dtype=x.dtype)
        _, o_t = jax.lax.scan(step, S0, (tb(q), tb(k), tb(v), tb(g), tb(beta)))
        out = jnp.moveaxis(o_t, 0, 1)
        gate = (x @ Wga.T @ Wgb.T).reshape(B, T, H, D)
        out = _rmsn(out, EPS_NORM) * o_norm_w * jax.nn.sigmoid(gate)
        return out.reshape(B, T, H * D) @ Wo.T

    def _L0_ffn_ref(x, gate_w, wg, wu, wd, sg, su, sd):
        import jax, jax.numpy as jnp
        import numpy as np
        DIM = 256
        INTER = 128
        E = 8
        TOP_K = 2
        ROUTE_SCALE = 1.0
        B, S, D = x.shape
        xf = x.reshape(-1, D)
        N = xf.shape[0]
        scores = jax.nn.softmax(xf @ gate_w.T, axis=-1)
        _, idx = jax.lax.top_k(scores, TOP_K)
        weights = jnp.take_along_axis(scores, idx, axis=-1) * ROUTE_SCALE
        cw = jnp.zeros((N, E), dtype=xf.dtype)
        cw = cw.at[jnp.arange(N)[:, None], idx].add(weights)
        g = jnp.einsum('nd,efd->nef', xf, wg)
        u = jnp.einsum('nd,efd->nef', xf, wu)
        h = jax.nn.silu(g) * u
        y = jnp.einsum('nef,edf->ned', h, wd)
        routed = jnp.einsum('ned,ne->nd', y, cw)
        shared = jax.nn.silu(xf @ sg.T) * (xf @ su.T) @ sd.T
        return (routed + shared).reshape(B, S, D)
    x = L0_attn_x
    x = x + _L0_attn_ref(_layernorm(x, axis=-1), L0_attn_Wq, L0_attn_Wk, L0_attn_Wv, L0_attn_wq_conv, L0_attn_wk_conv, L0_attn_wv_conv, L0_attn_Wfa, L0_attn_Wfb, L0_attn_Wb, L0_attn_Wga, L0_attn_Wgb, L0_attn_A_log, L0_attn_dt_bias, L0_attn_o_norm_w, L0_attn_Wo)
    x = x + _L0_ffn_ref(_layernorm(x, axis=-1), L0_ffn_gate_w, L0_ffn_wg, L0_ffn_wu, L0_ffn_wd, L0_ffn_sg, L0_ffn_su, L0_ffn_sd)
    return x

_drawn_inputs = setup_inputs


def setup_inputs(seed=0):
    import zlib

    import numpy as np

    out = dict(_drawn_inputs(seed))
    spreads = {'L0_attn_dt_bias': (0.0, 0.8), 'L0_attn_o_norm_w': (1.0, 0.6)}
    factors = {'L0_attn_Wfa': 8.0,
     'L0_attn_Wfb': 8.0,
     'L0_attn_Wb': 8.0,
     'L0_attn_Wga': 8.0,
     'L0_attn_Wgb': 8.0,
     'L0_attn_A_log': 8.0}
    for name, (base, spread) in spreads.items():
        noise = np.random.default_rng([zlib.crc32(name.encode()), seed]).standard_normal(out[name].shape)
        drawn = base * np.exp(spread * noise) if base else spread * noise
        out[name] = jnp.asarray(drawn.astype(out[name].dtype))
    for name, factor in factors.items():
        out[name] = (out[name] * factor).astype(out[name].dtype)
    return out
```

```python
from contextlib import ExitStack

import concourse.bass as bass
from concourse import mybir

ALU = mybir.AluOpType
ACT = mybir.ActivationFunctionType
F32 = mybir.dt.float32
U32 = mybir.dt.uint32
EXP_SET, LN_SET = "exp_and_others", "natural_log"
AX_X = mybir.AxisListType.X

P = 128
BATCH, SEQ, HID = 16, 512, 256
HEADS, TAPS = 8, 4
EXPERTS = 8
KT = HID // P
NCH = SEQ // P
HALF = P // 2
LEVELS = 7
NHEAD = BATCH * HEADS
EPS_QK, EPS_NORM, EPS_LN = 1e-6, 1e-5, 1e-5

QKV = 0
FB = QKV + KT * 3 * P
GB = FB + P
CONV = GB + P
DT = CONV + 3 * TAPS
ALOG = DT + 1
PAR = ALOG + 1

TOT_AT = [None]
_at = 0
for _l in range(1, LEVELS + 1):
    TOT_AT.append(_at)
    _at += SEQ >> _l
TOT_LEN = _at



def halves(ap, h):
    return ap.rearrange("p (m two h) -> p m two h", two=2, h=h)


def after(eng, sem, value):
    if isinstance(value, int) and value <= 0:
        return
    eng.wait_ge(sem, value)


def delta_moe(nc, x, params, wfa, wga, wb, wo, onw, gate_w, ffn_w, out):
    with ExitStack() as ctx:
        def sb(name, shape, dt=F32):
            return ctx.enter_context(nc.sbuf_tensor(name, shape, dt))

        def sem(name):
            return ctx.enter_context(nc.semaphore(name))

        bank = [ctx.enter_context(nc.psum_tensor(f"bank{n}", [P, 512], F32)) for n in range(8)]
        b_q, b_k, b_v, b_lvl, b_x, b_y, b_s, b_o = bank

        xall = sb("xall", [P, BATCH * NCH * HID])
        par = [sb(f"par{p}", [P, PAR]) for p in range(2)]
        wo_sb = sb("wo_sb", [P, HEADS * HID])
        onw_sb = sb("onw_sb", [P, 1])
        wfa_sb = sb("wfa_sb", [P, KT * P])
        wga_sb = sb("wga_sb", [P, KT * P])
        wb_sb = sb("wb_sb", [P, KT * HEADS])
        gw_sb = sb("gw_sb", [P, KT * EXPERTS])
        ident4 = sb("ident4", [P, SEQ])
        ident = ident4[:, 0:P]
        ones = sb("ones", [P, 1])
        plus_half = sb("plus_half", [P, NCH])
        minus_half = sb("minus_half", [P, NCH])
        mask = [sb(f"mask{l}", [P, NCH * HALF]) for l in range(LEVELS)]
        lower = sb("lower", [P, EXPERTS * EXPERTS])
        stats = sb("stats", [P, NCH * 6])
        mv = sb("mv", [P, NCH * 2])
        rstd = sb("rstd", [P, NCH])
        xn = sb("xn", [P, NCH * HID])
        xT = sb("xT", [P, KT * SEQ])
        faT = sb("faT", [P, SEQ])
        gaT = sb("gaT", [P, SEQ])
        bexp = sb("bexp", [P, NCH * HEADS])
        beta = sb("beta", [P, HEADS * NCH])
        y3 = [sb(f"y{n}", [P, SEQ]) for n in "qkv"]
        q = [sb(f"q{p}", [P, SEQ]) for p in range(2)]
        k = [sb(f"k{p}", [P, SEQ]) for p in range(2)]
        v = [sb(f"v{p}", [P, SEQ]) for p in range(2)]
        a = [sb(f"a{p}", [P, SEQ]) for p in range(2)]
        e_sb = sb("e_sb", [P, SEQ])
        w_sb = sb("w_sb", [P, SEQ])
        m_sb = sb("m_sb", [P, SEQ])
        amp = [sb(f"amp{p}", [P, 1]) for p in range(2)]
        sg = [sb(f"sg{p}", [P, SEQ]) for p in range(2)]
        tk = [sb(f"tk{p}", [P, 8]) for p in range(2)]
        dg = [sb(f"dg{p}", [P, NCH]) for p in range(2)]
        rec = sb("rec", [P, NCH])
        sc = [sb(f"sc{p}", [P, NCH]) for p in range(2)]
        rinv = [sb(f"rinv{p}", [P, NCH]) for p in range(2)]
        eo = [sb(f"eo{p}", [P, NCH]) for p in range(2)]
        tot = [sb(f"tot{p}", [P, TOT_LEN]) for p in range(2)]
        kq = [sb(f"kq{p}", [P, 2 * SEQ]) for p in range(2)]
        kl = sb("kl", [P, SEQ])
        lx = sb("lx", [P, 2 * LEVELS * SEQ])
        LT = [lx[:, l * SEQ:(l + 1) * SEQ] for l in range(LEVELS)]
        XS = [lx[:, (LEVELS + l) * SEQ:(LEVELS + l + 1) * SEQ] for l in range(LEVELS)]
        T = sb("T", [P, SEQ])
        TT = [sb(f"TT{p}", [P, SEQ]) for p in range(2)]
        AT = [sb(f"AT{p}", [P, SEQ]) for p in range(2)]
        kT = [sb(f"kT{p}", [P, 3 * P]) for p in range(2)]
        vs = [sb(f"vs{p}", [P, SEQ]) for p in range(2)]
        R = sb("R", [P, P])
        W = sb("W", [P, P])
        S = [sb(f"S{p}", [P, P]) for p in range(2)]
        junk = sb("junk", [P, P])
        ss = sb("ss", [P, NCH])
        zz = sb("zz", [P, NCH])
        nrm = sb("nrm", [P, NCH])
        og = sb("og", [P, SEQ])
        ogT = sb("ogT", [P, SEQ])

        names = """halves_ok pool_go dve_go sp_go x_in w_in consts ident_ok zero_ok wo_ok par_in0 par_in1 amp_ok
        bn_st bn_mv bn_var bn_rs xn_ok xnT_mm xt_ev fa_mm ga_mm be_mm fa_ev ga_ev be_ev be_one beta_ok
        q_mm k_mm v_mm f_mm g_mm tap0 dtap conv_done silu_done sq_done qk_prod
        fabs e_done f_read w_done nr_done ln_done t1_done t2_done decay_done sg_done
        sums_mm tk_done raw_done rec_done sc_done rinv_done tot_step tot_done
        kq_ready kl_ready kcopy lvl_mm lt_done qk_ev at_init t_init tt_init t_upd tt_upd
        x_mm x_ev y_mm vt_mm vt_ev kt_mm kt_ev
        ks_mm r_done z_mm w_ev su_mm s_ready o_mm osq z_done nrm_done og_done
        ogt_mm ogt_ev out_mm x2_add
        mask_step f_w f_st f_mv f_var f_rs f_xn f_xT_mm f_xT_ev r_mm r_max r_sub r_exp r_sum r_rec r_sc
        r_gt r_eq r_eql r_any r_rank r_cw g2_mm u2_mm silu2 h2 d_mm acc stored""".split()
        s = {n: sem(n) for n in names}
        par_in = [s["par_in0"], s["par_in1"]]

        def chunk(t, n, w=P):
            return t[:, n * w:(n + 1) * w]

        def tot_view(p, level):
            return a[p][:, :] if level == 0 else tot[p][:, TOT_AT[level]:TOT_AT[level] + (SEQ >> level)]

        block = ctx.enter_context(nc.Block())

        def supersteps(eng, batch_stage, step):
            def pair(j, bt, bc, ha, hc, A=True, B=(True, True), C=(True, True)):
                for p in range(2):
                    step(2 * j + p, j, p, bt, bc, ha + p, hc + p, A, B[p], C[p])
            last = BATCH - 1
            batch_stage(0)
            pair(0, 0, 0, 0, 0, True, (False, True), (False, False))
            pair(1, 0, 0, 2, 0)
            with eng.Fori(2, HEADS // 2) as hp:
                pair(hp, 0, 0, hp * 2, hp * 2 - 2)
            with eng.Fori(1, BATCH) as b:
                batch_stage(b)
                pair(b * (HEADS // 2), b, b - 1, 0, HEADS - 2)
                with eng.Fori(1, HEADS // 2) as hp:
                    pair(b * (HEADS // 2) + hp, b, b, hp * 2, hp * 2 - 2)
            pair(NHEAD // 2, last, last, 0, HEADS - 2, False, (True, False), (True, True))

        @block.sync
        def _(sp):
            for src, dst in ((wfa, wfa_sb), (wga, wga_sb), (wb, wb_sb), (wo, wo_sb), (onw, onw_sb), (gate_w, gw_sb)):
                sp.dma_start(dst[:, :], src).then_inc(s["w_in"], 16)
            xt = x.rearrange("b (n p) d -> p (b n) d", p=P)
            for b in range(BATCH):
                sp.dma_start(xall[:, b * NCH * HID:(b + 1) * NCH * HID].rearrange("p (n d) -> p n d", d=HID),
                             xt[:, b * NCH:(b + 1) * NCH, :]).then_inc(s["x_in"], 16)
                if b == 0:
                    for p in range(2):
                        sp.dma_start(par[p][:, :], params[p]).then_inc(par_in[p], 16)
                sp.wait_ge(s["x_in"], 16 * (b + 1))

            def load(i, p, h):
                for done, value in (("g_mm", i - 1), ("conv_done", 3 * (i - 1)), ("f_read", i - 1), ("decay_done", i - 1)):
                    sp.wait_ge(s[done], value)
                    sp.sem_inc(s["sp_go"], 1)
                sp.dma_start(par[p][:, :], params[h]).then_inc(par_in[p], 16)

            with sp.Fori(1, HEADS // 2) as hp:
                for p in range(2):
                    load(2 * hp + p, p, 2 * hp + p)
            with sp.Fori(1, BATCH) as b:
                with sp.Fori(0, HEADS // 2) as hp:
                    for p in range(2):
                        load(b * HEADS + 2 * hp + p, p, 2 * hp + p)
            sp.wait_ge(s["x_mm"], LEVELS * NHEAD)
            sp.wait_ge(s["y_mm"], (LEVELS - 1) * NHEAD)
            sp.wait_ge(s["x_ev"], (LEVELS - 1) * NHEAD)
            sp.wait_ge(s["tt_upd"], LEVELS * NHEAD)
            sp.dma_start(lx[:, 0:(EXPERTS + 1) * 3 * HID], ffn_w).then_inc(s["f_w"], 16)
            ot = out.rearrange("b (n p) d -> p (b n) d", p=P)
            with sp.Fori(0, BATCH) as m:
                sp.wait_ge(s["acc"], (m + 1) * (EXPERTS + 1) * NCH)
                sp.sem_inc(s["sp_go"], 1)
                sp.dma_start(ot[:, bass.ds(m * NCH, NCH), :],
                             xall[:, bass.ds(m * (NCH * HID), NCH * HID)].rearrange("p (n d) -> p n d", d=HID)
                             ).then_inc(s["stored"], 16)
            sp.wait_ge(s["stored"], 16 * BATCH)

        @block.gpsimd
        def _(pool):
            pool.memset(ident4[:, :], 0.0).then_inc(s["mask_step"], 1)
            pool.wait_ge(s["mask_step"], 1)
            pool.affine_select(out=ident4[:, :].rearrange("p (n c) -> p n c", c=P),
                               in_=ident4[:, :].rearrange("p (n c) -> p n c", c=P), compare_op=ALU.not_equal,
                               fill=1.0, base=0, pattern=[[0, NCH], [-1, P]], channel_multiplier=1
                               ).then_inc(s["ident_ok"], 1)
            pool.memset(ones[:, :], 1.0).then_inc(s["consts"], 1)
            pool.memset(plus_half[:, :], 0.5).then_inc(s["halves_ok"], 1)
            pool.memset(minus_half[:, :], -0.5).then_inc(s["halves_ok"], 1)
            pool.wait_ge(s["halves_ok"], 2)
            steps = 1
            for l in range(LEVELS):
                h, m = 1 << l, HALF >> l
                mv4 = mask[l][:, :].rearrange("p (n m h) -> p n m h", n=NCH, h=h)
                pool.memset(mask[l][:, :], 1.0).then_inc(s["mask_step"], 1)
                steps += 1
                pool.wait_ge(s["mask_step"], steps)
                pool.affine_select(out=mv4, in_=mv4, compare_op=ALU.is_ge, fill=0.0, base=0,
                                   pattern=[[0, NCH], [-2 * h, m], [0, h]], channel_multiplier=1
                                   ).then_inc(s["mask_step"], 1)
                steps += 1
                pool.wait_ge(s["mask_step"], steps)
                pool.affine_select(out=mv4, in_=mv4, compare_op=ALU.is_ge, fill=0.0, base=h - 1,
                                   pattern=[[0, NCH], [2 * h, m], [0, h]], channel_multiplier=-1
                                   ).then_inc(s["consts"], 1)
            pool.memset(lower[:, :], 1.0).then_inc(s["mask_step"], 1)
            pool.wait_ge(s["mask_step"], steps + 1)
            lo = lower[:, :].rearrange("p (e f) -> p e f", f=EXPERTS)
            pool.affine_select(out=lo, in_=lo, compare_op=ALU.is_gt, fill=0.0, base=0,
                               pattern=[[1, EXPERTS], [-1, EXPERTS]], channel_multiplier=0).then_inc(s["consts"], 1)

            def step(i, j, p, bt, bc, ha, hc, A, B, C):
                iB, iC, pB = i - 1, i - 2, 1 - p

                def kl_update(l):
                    h = 1 << l
                    pool.wait_ge(s["lvl_mm"], LEVELS * iB + l + 1)
                    if l == 0:
                        after(pool, s["kt_mm"], iB)
                        src = halves(k[pB][:, :], h)[:, :, 0, :]
                        pool.wait_ge(s["silu_done"], 3 * iB + 2)
                    else:
                        pool.wait_ge(s["kl_ready"], LEVELS * iB + l)
                        if l == 1:
                            pool.wait_ge(s["kcopy"], iB + 1)
                        src = halves(kl[:, :], h)[:, :, 0, :]
                    totr = tot_view(pB, l).rearrange("p (m two) -> p m two", two=2)[:, :, 1:2]
                    pool.tensor_tensor(halves(kl[:, :], h)[:, :, 0, :], src,
                                       totr.broadcast_to([P, SEQ // (2 * h), h]), ALU.mult
                                       ).then_inc(s["kl_ready"], 1)

                if B:
                    after(pool, s["x_mm"], LEVELS * iB)
                    after(pool, s["t_upd"], (LEVELS - 1) * iB)
                    pool.sem_inc(s["pool_go"], 1)
                    pool.tensor_copy(T[:, :], ident4[:, :]).then_inc(s["t_init"], 1)
                    after(pool, s["z_mm"], NCH * (iB - 1))
                    pool.sem_inc(s["pool_go"], 1)
                    pool.tensor_copy(TT[pB][:, :], ident4[:, :]).then_inc(s["tt_init"], 1)
                    pool.wait_ge(s["tot_done"], iB + 1)
                    for l in range(4):
                        kl_update(l)
                if A:
                    pool.wait_ge(s["ln_done"], i + 1)
                    pool.tensor_tensor(e_sb[:, :], e_sb[:, :], w_sb[:, :], ALU.subtract).then_inc(s["t1_done"], 1)
                    pool.wait_ge(s["t1_done"], i + 1)
                    pool.wait_ge(s["f_read"], i + 1)
                    pool.tensor_tensor(e_sb[:, :], e_sb[:, :], m_sb[:, :], ALU.subtract).then_inc(s["t2_done"], 1)
                if B:
                    kl_update(4)
                if C:
                    pool.wait_ge(s["z_done"], iC + 1)
                    after(pool, s["og_done"], iC)
                    pool.tensor_tensor(nrm[:, :], zz[:, :], minus_half[:, :], ALU.pow).then_inc(s["nrm_done"], 1)
                if B:
                    kl_update(5)
                if A:
                    pool.wait_ge(s["decay_done"], i + 1)
                    after(pool, s["s_ready"], 3 * (i - 1))
                    for l in range(1, LEVELS + 1):
                        if l > 1:
                            pool.wait_ge(s["tot_step"], (LEVELS - 1) * i + l - 1)
                        two = tot_view(p, l - 1).rearrange("p (m two) -> p m two", two=2)
                        pool.tensor_tensor(tot_view(p, l).unsqueeze(2), two[:, :, 0:1], two[:, :, 1:2], ALU.mult
                                           ).then_inc(s["tot_step" if l < LEVELS else "tot_done"], 1)
                    pool.wait_ge(s["silu_done"], 3 * i + 3)
                    pool.tensor_tensor(y3[2][:, :], q[p][:, :], k[p][:, :], ALU.mult).then_inc(s["qk_prod"], 1)
                if B:
                    kl_update(6)
                if A:
                    pool.wait_ge(s["tk_done"], i + 1)
                    after(pool, s["vt_ev"], i - 1)
                    pool.tensor_tensor(rinv[p][:, :], tk[p][:, 4:8], plus_half[:, :], ALU.pow).then_inc(s["rinv_done"], 1)

            def rstd_of(var, rs, m):
                pool.wait_ge(s[var], m + 1)
                pool.tensor_tensor(rstd[:, :], rstd[:, :], minus_half[:, :], ALU.pow).then_inc(s[rs], 1)

            supersteps(pool, lambda bn: rstd_of("bn_var", "bn_rs", bn), step)
            rstd_of("f_var", "f_rs", 0)
            with pool.Fori(1, BATCH) as m:
                rstd_of("f_var", "f_rs", m)

        @block.scalar
        def _(act):
            act.preload_act_table_set(EXP_SET)
            def batch_stage(bn):
                for t in range(KT):
                    act.wait_ge(s["xnT_mm"], KT * bn + t + 1)
                    act.activation(chunk(xT, t, SEQ), bank[t][:, :], ACT.Copy).then_inc(s["xt_ev"], 1)
                act.wait_ge(s["fa_mm"], bn + 1)
                act.activation(faT[:, :], b_v[:, :], ACT.Copy).then_inc(s["fa_ev"], 1)
                act.wait_ge(s["ga_mm"], bn + 1)
                act.activation(gaT[:, :], b_q[:, :], ACT.Copy).then_inc(s["ga_ev"], 1)
                act.wait_ge(s["be_mm"], bn + 1)
                after(act, s["beta_ok"], bn)
                act.activation(bexp[:, :], b_k[:, 0:NCH * HEADS], ACT.Exp, scale=-1.0).then_inc(s["be_ev"], 1)

            def step(i, j, p, bt, bc, ha, hc, A, B, C):
                iB, iC, pB = i - 1, i - 2, 1 - p

                def tap0(t, mm):
                    act.wait_ge(s[mm], i + 1)
                    if t == 0:
                        act.wait_ge(par_in[p], 16 * (j + 1))
                        after(act, s["sums_mm"], i)
                    at = CONV + t * TAPS + TAPS - 1
                    act.activation(y3[t][:, :], bank[t][:, :], ACT.Copy, scale=par[p][:, at:at + 1]
                                   ).then_inc(s["tap0"], 1)

                def x_evict(l):
                    h = 1 << l
                    act.wait_ge(s["x_mm"], LEVELS * iB + l + 1)
                    after(act, s["y_mm"], (LEVELS - 1) * iB - (LEVELS - 1) + l)
                    if l == 1:
                        act.wait_ge(s["zero_ok"], 1)
                    act.activation(halves(XS[l], h)[:, :, 0, :],
                                   b_x[:, 0:NCH * HALF].rearrange("p (m h) -> p m h", h=h), ACT.Copy
                                   ).then_inc(s["x_ev"], 1)

                def w_evict(n):
                    act.wait_ge(s["z_mm"], NCH * iC + n + 1)
                    act.wait_ge(s["sc_done"], iC + 1)
                    act.activation(W[:, :], b_s[:, P:2 * P], ACT.Copy, scale=sc[p][:, n:n + 1]).then_inc(s["w_ev"], 1)

                def turned_v():
                    act.wait_ge(s["vt_mm"], iB + 1)
                    act.wait_ge(s["rinv_done"], iB + 1)
                    after(act, s["o_mm"], NCH * (iB - 1))
                    for n in range(NCH):
                        ins = act.activation(chunk(vs[pB], n), chunk(b_v, n), ACT.Copy, scale=rinv[pB][:, n:n + 1])
                    ins.then_inc(s["vt_ev"], 1)

                for slot in range(8):
                    if slot == 0 and B:
                        after(act, s["kt_mm"], iB)
                        act.activation(halves(kl[:, :], 1)[:, :, 1, :], halves(k[pB][:, :], 1)[:, :, 1, :], ACT.Copy
                                       ).then_inc(s["kcopy"], 1)
                    if slot == 0 and C:
                        w_evict(0)
                    if slot == 3 and A:
                        act.wait_ge(s["f_mm"], i + 1)
                        after(act, s["t2_done"], i)
                        act.activation(e_sb[:, :], b_q[:, :], ACT.Abs, bias=par[p][:, DT:DT + 1]).then_inc(s["fabs"], 1)
                        act.wait_ge(s["fabs"], i + 1)
                        act.activation(e_sb[:, :], e_sb[:, :], ACT.Exp, scale=-1.0).then_inc(s["e_done"], 1)
                        act.activation(amp[p][:, :], par[p][:, ALOG:ALOG + 1], ACT.Exp).then_inc(s["amp_ok"], 1)
                        act.preload_act_table_set(LN_SET)
                    if slot == 5 and A:
                        act.wait_ge(s["t2_done"], i + 1)
                        act.wait_ge(s["amp_ok"], i + 1)
                        after(act, s["tot_done"], i - 1)
                        act.activation(a[p][:, :], e_sb[:, :], ACT.Exp, scale=amp[p][:, 0:1]
                                       ).then_inc(s["decay_done"], 1)
                    if slot == 5 and A:
                        after(act, s["lvl_mm"], LEVELS * (i - 1))
                        after(act, s["kl_ready"], LEVELS * (i - 1))
                        after(act, s["vt_mm"], i - 1)
                        for t, dst in enumerate((q, k, v)):
                            act.wait_ge(s["conv_done"], 3 * i + t + 1)
                            act.activation(dst[p][:, :], y3[t][:, :], ACT.Silu).then_inc(s["silu_done"], 1)
                    if slot == 7 and C:
                        act.wait_ge(s["ogt_mm"], iC + 1)
                        after(act, s["out_mm"], 2 * iC)
                        act.activation(ogT[:, :], b_k[:, :], ACT.Copy).then_inc(s["ogt_ev"], 1)
                    if B and slot >= 2:
                        x_evict(slot - 1)
                    if slot < 3 and A:
                        tap0(slot, ("q_mm", "k_mm", "v_mm")[slot])
                    if 1 <= slot <= 3 and C:
                        w_evict(slot)
                    if slot == 4:
                        if A:
                            act.wait_ge(s["nr_done"], i + 1)
                            act.activation(w_sb[:, :], w_sb[:, :], ACT.Ln).then_inc(s["ln_done"], 1)
                            act.preload_act_table_set(EXP_SET)
                        if C:
                            act.wait_ge(s["o_mm"], NCH * (iC + 1))
                            after(act, s["z_done"], iC)
                            for n in range(NCH):
                                if n:
                                    act.wait_ge(s["osq"], NCH * iC + n)
                                act.activation(junk[:, :], chunk(b_o, n), ACT.Square, accum_out=ss[:, n:n + 1]
                                               ).then_inc(s["osq"], 1)
                        if B:
                            turned_v()
                    if slot == 5:
                        if A:
                            act.wait_ge(s["g_mm"], i + 1)
                            after(act, s["og_done"], i - 1)
                            act.activation(sg[p][:, :], b_k[:, :], ACT.Sigmoid).then_inc(s["sg_done"], 1)
                            act.preload_act_table_set(EXP_SET)
                    if slot == 6 and A:
                        for t, src in enumerate((q, k)):
                            act.wait_ge(s["silu_done"], 3 * i + t + 1)
                            act.activation(y3[t][:, :], src[p][:, :], ACT.Square).then_inc(s["sq_done"], 1)
                    if slot == 7:
                        if B:
                            act.wait_ge(s["kt_mm"], iB + 1)
                            act.activation(kT[pB][:, :], b_x[:, 0:3 * P], ACT.Copy).then_inc(s["kt_ev"], 1)

            supersteps(act, batch_stage, step)

            def ffn_block(m):
                act.preload_act_table_set(EXP_SET)
                for t in range(KT):
                    act.wait_ge(s["f_xT_mm"], KT * m + t + 1)
                    act.activation(chunk(xT, t, SEQ), bank[t][:, :], ACT.Copy).then_inc(s["f_xT_ev"], 1)
                act.wait_ge(s["r_sub"], m + 1)
                act.activation(bexp[:, :], bexp[:, :], ACT.Exp).then_inc(s["r_exp"], 1)
                for e in range(EXPERTS + 1):
                    n = m * (EXPERTS + 1) + e
                    act.wait_ge(s["g2_mm"], n + 1)
                    after(act, s["h2"], n - 1 if (e > 1 or isinstance(m, int)) else n - 1)
                    act.activation(q[e % 2][:, :], bank[3 + 2 * (e % 2)][:, :], ACT.Silu).then_inc(s["silu2"], 1)

            ffn_block(0)
            with act.Fori(1, BATCH) as m:
                ffn_block(m)

        @block.vector
        def _(dve):
            dve.memset(lx[:, :], 0.0).then_inc(s["zero_ok"], 1)
            dve.wait_ge(s["w_in"], 16 * 6)
            dve.tensor_scalar(wo_sb[:, :], wo_sb[:, :], onw_sb[:, 0:1], None, ALU.mult).then_inc(s["wo_ok"], 1)
            dve.wait_ge(s["consts"], 2 + LEVELS)
            dve.wait_ge(s["ident_ok"], 1)
            dve.wait_ge(s["zero_ok"], 1)

            def layernorm(m, st, mvs, var, rs, done, waits):
                for n in range(NCH):
                    ins = dve.bn_stats(chunk(stats, n, 6), xall[:, bass.ds(m * (NCH * HID) + n * HID, HID)])
                ins.then_inc(s[st], 1)
                dve.wait_ge(s[st], m + 1)
                dve.sem_inc(s["dve_go"], 1)
                for n in range(NCH):
                    ins = dve.bn_aggr(chunk(mv, n, 2), chunk(stats, n, 6))
                ins.then_inc(s[mvs], 1)
                dve.wait_ge(s[mvs], m + 1)
                dve.tensor_scalar(rstd[:, :].unsqueeze(2),
                                  mv[:, :].rearrange("p (n two) -> p n two", two=2)[:, :, 1:2],
                                  EPS_LN, None, ALU.add).then_inc(s[var], 1)
                dve.wait_ge(s[rs], m + 1)
                for sem_, value in waits:
                    after(dve, s[sem_], value)
                for n in range(NCH):
                    ins = dve.tensor_scalar(chunk(xn, n, HID), xall[:, bass.ds(m * (NCH * HID) + n * HID, HID)],
                                            mv[:, 2 * n:2 * n + 1], rstd[:, n:n + 1], ALU.subtract, ALU.mult)
                ins.then_inc(s[done], 1)

            def batch_stage(bn):
                dve.wait_ge(s["x_in"], bn * 16 + 16)
                layernorm(bn, "bn_st", "bn_mv", "bn_var", "bn_rs", "xn_ok", [("xnT_mm", KT * bn)])
                dve.wait_ge(s["be_ev"], bn + 1)
                dve.tensor_scalar(bexp[:, :], bexp[:, :], 1.0, None, ALU.add).then_inc(s["be_one"], 1)
                dve.wait_ge(s["be_one"], bn + 1)
                dve.reciprocal(beta[:, :].rearrange("p (h n) -> p n h", n=NCH),
                               bexp[:, :].rearrange("p (n h) -> p n h", h=HEADS)).then_inc(s["beta_ok"], 1)

            def step(i, j, p, bt, bc, ha, hc, A, B, C):
                iB, iC, pB = i - 1, i - 2, 1 - p

                def l_evict(l):
                    h = 1 << l
                    dve.wait_ge(s["lvl_mm"], LEVELS * iB + l + 1)
                    if l == 0:
                        dve.wait_ge(s["sc_done"], iB + 1)
                    after(dve, s["x_mm"], LEVELS * iB - LEVELS + l + 1)
                    for n in range(NCH):
                        ins = dve.scalar_tensor_tensor(
                            out=halves(chunk(LT[l], n), h)[:, :, 1, :],
                            in0=b_lvl[:, n * HALF:(n + 1) * HALF].rearrange("p (m h) -> p m h", h=h),
                            scalar=sc[pB][:, n:n + 1],
                            in1=mask[l][:, 0:HALF].rearrange("p (m h) -> p m h", h=h), op0=ALU.mult, op1=ALU.mult)
                    ins.then_inc(s["lt_done"], 1)

                def kq_update(l):
                    h = 1 << l
                    m = SEQ // (2 * h)
                    dve.wait_ge(s["kq_ready"], (LEVELS + 1) * iB + l + 1)
                    if l == 0:
                        dve.wait_ge(s["tot_done"], iB + 1)
                    totl = tot_view(pB, l).rearrange("p (m two) -> p m two", two=2)[:, :, 0:1]
                    for part in range(2):
                        view = halves(chunk(kq[pB], part, SEQ), h)[:, :, 1, :]
                        ins = dve.tensor_tensor(view, view, totl.broadcast_to([P, m, h]), ALU.mult)
                    ins.then_inc(s["kq_ready"], 1)

                def qk_evict(l):
                    h = 1 << l
                    if l == 0:
                        dve.wait_ge(s["at_init"], iB + 1)
                    else:
                        dve.wait_ge(s["qk_ev"], LEVELS * iB + l)
                    dve.sem_inc(s["dve_go"], 1)
                    dve.copy_predicated(halves(AT[pB][:, :], h)[:, :, 1, :],
                                        mask[l][:, :].bitcast(U32).rearrange("p (m h) -> p m h", h=h),
                                        b_lvl[:, 256:512].rearrange("p (m h) -> p m h", h=h)).then_inc(s["qk_ev"], 1)

                def t_update(l):
                    h = 1 << l
                    tl = halves(T[:, :], h)[:, :, 0, :]
                    tr = halves(TT[pB][:, :], h)[:, :, 1, :]
                    if l == 0:
                        dve.wait_ge(s["t_init"], iB + 1)
                        dve.wait_ge(s["tt_init"], iB + 1)
                        dve.wait_ge(s["x_mm"], LEVELS * iB + 1)
                        dve.wait_ge(s["lt_done"], LEVELS * iB + 1)
                        dve.tensor_tensor(tl, tl, b_x[:, 0:256].rearrange("p (m h) -> p m h", h=h),
                                          ALU.subtract).then_inc(s["t_upd"], 1)
                        dve.tensor_tensor(tr, tr, halves(LT[0], h)[:, :, 1, :], ALU.subtract).then_inc(s["tt_upd"], 1)
                        return
                    dve.wait_ge(s["y_mm"], (LEVELS - 1) * iB + l)
                    if l < LEVELS - 1:
                        dve.wait_ge(s["t_upd"], (LEVELS - 1) * iB + l)
                        dve.tensor_tensor(tl, tl, b_y[:, 0:256].rearrange("p (m h) -> p m h", h=h),
                                          ALU.subtract).then_inc(s["t_upd"], 1)
                    dve.wait_ge(s["tt_upd"], LEVELS * iB + l)
                    dve.tensor_tensor(tr, tr, b_y[:, 256:512].rearrange("p (m h) -> p m h", h=h),
                                      ALU.subtract).then_inc(s["tt_upd"], 1)

                def conv(t):
                    dve.wait_ge(s["tap0"], 3 * i + t + 1)
                    for d in range(1, TAPS):
                        at = CONV + t * TAPS + TAPS - 1 - d
                        if d > 1:
                            dve.wait_ge(s["dtap"], 2 * (3 * i + t) + d - 1)
                        ins = dve.scalar_tensor_tensor(out=y3[t][:, d:SEQ], in0=bank[t][:, 0:SEQ - d],
                                                       scalar=par[p][:, at:at + 1], in1=y3[t][:, d:SEQ],
                                                       op0=ALU.mult, op1=ALU.add)
                        ins.then_inc(s["dtap" if d < TAPS - 1 else "conv_done"], 1)

                def s_update(n):
                    dve.wait_ge(s["su_mm"], 3 * iC + n + 1)
                    su = b_s[:, 2 * P:3 * P]
                    if n == 0:
                        dve.tensor_copy(S[0][:, :], su).then_inc(s["s_ready"], 1)
                        return
                    if n == 1:
                        dve.wait_ge(s["tot_done"], iC + 1)
                    dve.wait_ge(s["s_ready"], 3 * iC + n)
                    dve.scalar_tensor_tensor(out=S[n % 2][:, :], in0=S[(n - 1) % 2][:, :],
                                             scalar=tot_view(p, LEVELS)[:, n:n + 1], in1=su,
                                             op0=ALU.mult, op1=ALU.add).then_inc(s["s_ready"], 1)

                def residual(n):
                    dve.wait_ge(s["ks_mm"], 3 * iC + n)
                    dve.wait_ge(s["vt_ev"], iC + 1)
                    dve.tensor_tensor(R[:, :], chunk(vs[p], n), b_s[:, 0:P], ALU.subtract).then_inc(s["r_done"], 1)

                def outputs():
                    dve.wait_ge(s["nrm_done"], iC + 1)
                    dve.wait_ge(s["sg_done"], iC + 1)
                    after(dve, s["ogt_mm"], iC)
                    for n in range(NCH):
                        ins = dve.scalar_tensor_tensor(out=chunk(og, n), in0=chunk(b_o, n),
                                                       scalar=nrm[:, n:n + 1], in1=chunk(sg[p], n),
                                                       op0=ALU.mult, op1=ALU.mult)
                    ins.then_inc(s["og_done"], 1)

                for slot in range(8):
                    if C and 1 <= slot <= 3:
                        s_update(slot - 1)
                    if B and slot < LEVELS:
                        l_evict(slot)
                        kq_update(slot)
                    if C and 1 <= slot <= 3:
                        residual(slot)
                    if B and slot < LEVELS:
                        qk_evict(slot)
                    if A and 1 <= slot <= 3:
                        conv(slot - 1)
                    if C and slot == 5:
                        outputs()
                    if A and slot == 7:
                        dve.wait_ge(s["sums_mm"], i + 1)
                        after(dve, s["rinv_done"], i - 1)
                        dve.tensor_scalar(tk[p][:, :], b_v[:, 0:8], P * EPS_QK, None, ALU.add).then_inc(s["tk_done"], 1)
                        dve.tensor_copy(dg[p][:, :], b_v[:, 8:12]).then_inc(s["raw_done"], 1)
                        dve.wait_ge(s["tk_done"], i + 1)
                        dve.reciprocal(rec[:, :], tk[p][:, 4:8]).then_inc(s["rec_done"], 1)
                        dve.tensor_scalar(eo[p][:, :], tk[p][:, 0:4], P * EPS_NORM, None, ALU.mult)
                        dve.wait_ge(s["rec_done"], i + 1)
                        dve.wait_ge(s["beta_ok"], bt + 1)
                        after(dve, s["w_ev"], NCH * (i - 1))
                        dve.tensor_tensor(sc[p][:, :], rec[:, :], beta[:, bass.ds(ha * NCH, NCH)], ALU.mult
                                          ).then_inc(s["sc_done"], 1)
                    if B and slot >= 1:
                        t_update(slot - 1)
                    if A and slot == 3:
                        dve.wait_ge(s["fabs"], i + 1)
                        after(dve, s["t2_done"], i)
                        dve.tensor_scalar(m_sb[:, :], b_q[:, :], par[p][:, DT:DT + 1], 0.0, ALU.add, ALU.max
                                          ).then_inc(s["f_read"], 1)
                        dve.wait_ge(s["e_done"], i + 1)
                        dve.tensor_scalar(w_sb[:, :], e_sb[:, :], 1.0, None, ALU.add).then_inc(s["w_done"], 1)
                        dve.wait_ge(s["w_done"], i + 1)
                        dve.scalar_tensor_tensor(out=e_sb[:, :], in0=w_sb[:, :], scalar=1.0, in1=e_sb[:, :],
                                                 op0=ALU.subtract, op1=ALU.subtract).then_inc(s["nr_done"], 1)
                    if C and slot == 4:
                        dve.wait_ge(s["osq"], NCH * (iC + 1))
                        after(dve, s["nrm_done"], iC)
                        dve.scalar_tensor_tensor(out=zz[:, :], in0=ss[:, :], scalar=1.0 / P, in1=eo[p][:, :],
                                                 op0=ALU.mult, op1=ALU.add).then_inc(s["z_done"], 1)
                    if A and slot == 6:
                        dve.wait_ge(s["decay_done"], i + 1)
                        after(dve, s["o_mm"], NCH * (i - 1))
                        dve.wait_ge(s["silu_done"], 3 * i + 2)
                        dve.tensor_tensor(chunk(kq[p], 1, SEQ), q[p][:, :], a[p][:, :], ALU.mult)
                        dve.tensor_tensor(chunk(kq[p], 0, SEQ), k[p][:, :], a[p][:, :], ALU.mult
                                          ).then_inc(s["kq_ready"], 1)
                    if A and slot == 7:
                        dve.wait_ge(s["raw_done"], i + 1)
                        for n in range(NCH):
                            ins = dve.tensor_scalar(chunk(AT[p], n), ident, dg[p][:, n:n + 1], None, ALU.mult)
                        ins.then_inc(s["at_init"], 1)
                    if C and slot == 7:
                        for half in range(2):
                            dve.wait_ge(s["out_mm"], 2 * iC + half + 1)
                            after(dve, s["x2_add"], 2 * iC + half - 1 if isinstance(iC, int) else 2 * iC + half)
                            at = bass.ds(bc * (NCH * HID) + half * 512, 512)
                            dve.tensor_tensor(xall[:, at], xall[:, at], bank[half][:, :], ALU.add
                                              ).then_inc(s["x2_add"], 1)

            supersteps(dve, batch_stage, step)

            def ffn_block(m):
                layernorm(m, "f_st", "f_mv", "f_var", "f_rs", "f_xn", [("f_xT_mm", KT * m)])
                E8 = [P, NCH, EXPERTS]
                lg = b_v[:, 0:NCH * EXPERTS].rearrange("p (n e) -> p n e", e=EXPERTS)
                ex = bexp[:, :].rearrange("p (n e) -> p n e", e=EXPERTS)
                score = beta[:, :].rearrange("p (n e) -> p n e", e=EXPERTS)
                gt = e_sb[:, 0:256].rearrange("p (n e f) -> p n e f", n=NCH, e=EXPERTS)
                eq = w_sb[:, 0:256].rearrange("p (n e f) -> p n e f", n=NCH, e=EXPERTS)
                e84 = [P, NCH, EXPERTS, EXPERTS]
                dve.wait_ge(s["r_mm"], m + 1)
                dve.tensor_reduce(rec[:, :], lg, AX_X, ALU.max).then_inc(s["r_max"], 1)
                dve.wait_ge(s["r_max"], m + 1)
                dve.tensor_tensor(ex, lg, rec[:, :].unsqueeze(2).broadcast_to(E8), ALU.subtract).then_inc(s["r_sub"], 1)
                dve.wait_ge(s["r_exp"], m + 1)
                dve.tensor_reduce(zz[:, :], ex, AX_X, ALU.add).then_inc(s["r_sum"], 1)
                dve.wait_ge(s["r_sum"], m + 1)
                dve.reciprocal(ss[:, :], zz[:, :]).then_inc(s["r_rec"], 1)
                dve.wait_ge(s["r_rec"], m + 1)
                dve.tensor_tensor(score, ex, ss[:, :].unsqueeze(2).broadcast_to(E8), ALU.mult).then_inc(s["r_sc"], 1)
                dve.wait_ge(s["r_sc"], m + 1)
                other = score.unsqueeze(2).broadcast_to(e84)
                own = score.unsqueeze(3).broadcast_to(e84)
                dve.tensor_tensor(gt, other, own, ALU.is_gt).then_inc(s["r_gt"], 1)
                dve.tensor_tensor(eq, other, own, ALU.is_equal).then_inc(s["r_eq"], 1)
                dve.wait_ge(s["r_eq"], m + 1)
                lows = lower[:, :].rearrange("p (e f) -> p e f", f=EXPERTS).unsqueeze(1).broadcast_to(e84)
                dve.tensor_tensor(eq, eq, lows, ALU.mult).then_inc(s["r_eql"], 1)
                dve.wait_ge(s["r_eql"], m + 1)
                dve.wait_ge(s["r_gt"], m + 1)
                dve.tensor_tensor(gt, gt, eq, ALU.add).then_inc(s["r_any"], 1)
                dve.wait_ge(s["r_any"], m + 1)
                dve.tensor_reduce(ex, gt, AX_X, ALU.add).then_inc(s["r_rank"], 1)
                dve.wait_ge(s["r_rank"], m + 1)
                dve.scalar_tensor_tensor(out=ex, in0=ex, scalar=1.5, in1=score, op0=ALU.is_lt, op1=ALU.mult
                                         ).then_inc(s["r_cw"], 1)
                dve.wait_ge(s["r_cw"], m + 1)

                def hidden(e):
                    n = m * (EXPERTS + 1) + e
                    dve.wait_ge(s["silu2"], n + 1)
                    dve.wait_ge(s["u2_mm"], n + 1)
                    after(dve, s["d_mm"], 2 * (n - 1))
                    dve.tensor_tensor(k[e % 2][:, :], q[e % 2][:, :], bank[4 + 2 * (e % 2)][:, :], ALU.mult
                                      ).then_inc(s["h2"], 1)

                def add(e):
                    n = m * (EXPERTS + 1) + e
                    for t in range(NCH):
                        if t % 2 == 0:
                            dve.wait_ge(s["d_mm"], 2 * n + t // 2 + 1)
                        after(dve, s["acc"], NCH * n + t - NCH + 1)
                        at = bass.ds(m * (NCH * HID) + t * HID, HID)
                        dve.scalar_tensor_tensor(
                            out=xall[:, at], in0=bank[7 if t < 2 else 2][:, (t % 2) * HID:(t % 2 + 1) * HID],
                            scalar=1.0 if e == EXPERTS else bexp[:, t * EXPERTS + e:t * EXPERTS + e + 1],
                            in1=xall[:, at], op0=ALU.mult, op1=ALU.add).then_inc(s["acc"], 1)

                hidden(0)
                for e in range(EXPERTS + 1):
                    if e < EXPERTS:
                        hidden(e + 1)
                    add(e)

            dve.wait_ge(s["x2_add"], 2 * NHEAD)
            ffn_block(0)
            with dve.Fori(1, BATCH) as m:
                ffn_block(m)

        @block.tensor
        def _(pe):
            pe.wait_ge(s["ident_ok"], 1)
            pe.wait_ge(s["consts"], 1)
            pe.wait_ge(s["w_in"], 16 * 6)
            pe.wait_ge(s["zero_ok"], 1)
            pe.wait_ge(s["wo_ok"], 1)

            def turn_x(dst_sem):
                for t in range(KT):
                    for n in range(NCH):
                        ins = pe.transpose(chunk(bank[t], n), xn[:, n * HID + t * P:n * HID + (t + 1) * P], ident)
                    ins.then_inc(s[dst_sem], 1)

            def batch_stage(bn):
                pe.wait_ge(s["xn_ok"], bn + 1)
                after(pe, s["x2_add"], 2 * (HEADS * bn - 2))
                turn_x("xnT_mm")
                pe.wait_ge(s["xt_ev"], KT * (bn + 1))
                after(pe, s["raw_done"], HEADS * bn)
                for w, dst, done in ((wfa_sb, b_v, "fa_mm"), (wga_sb, b_q, "ga_mm")):
                    for t in range(KT):
                        ins = pe.matmul(dst[:, :], chunk(w, t), chunk(xT, t, SEQ), start=t == 0, stop=t == KT - 1)
                    ins.then_inc(s[done], 1)
                for n in range(NCH):
                    for t in range(KT):
                        ins = pe.matmul(b_k[:, n * HEADS:(n + 1) * HEADS], xT[:, t * SEQ + n * P:t * SEQ + (n + 1) * P],
                                        chunk(wb_sb, t, HEADS), start=t == 0, stop=t == KT - 1)
                ins.then_inc(s["be_mm"], 1)

            def step(i, j, p, bt, bc, ha, hc, A, B, C):
                iB, iC, pB = i - 1, i - 2, 1 - p

                def project(t, done):
                    for kt in range(KT):
                        at = QKV + (kt * 3 + t) * P
                        ins = pe.matmul(bank[t][:, :], par[p][:, at:at + P], chunk(xT, kt, SEQ),
                                        start=kt == 0, stop=kt == KT - 1)
                    ins.then_inc(s[done], 1)

                def level(l):
                    h = 1 << l
                    pe.wait_ge(s["kq_ready"], (LEVELS + 1) * iB + l + 1)
                    if l:
                        pe.wait_ge(s["kl_ready"], LEVELS * iB + l)
                    if l == 1:
                        pe.wait_ge(s["kcopy"], iB + 1)
                    after(pe, s["qk_ev"], LEVELS * iB + l)
                    left = kl if l else k[pB]
                    right = kq[pB][:, :].rearrange("p (q n m two h) -> p q n m two h", q=2, n=NCH, two=2, h=h)
                    dst = b_lvl[:, :].rearrange("p (q n m h) -> p q n m h", q=2, n=NCH, h=h)
                    for n in range(NCH):
                        ins = pe.matmul(dst[:, :, n], chunk(left, n), right[:, :, n, :, 1, :], start=True, stop=True)
                    ins.then_inc(s["lvl_mm"], 1)

                def lt_times_t(l):
                    h = 1 << l
                    pe.wait_ge(s["lt_done"], LEVELS * iB + l + 1)
                    if l == 0:
                        pe.wait_ge(s["t_init"], iB + 1)
                        after(pe, s["kt_ev"], iB)
                    else:
                        pe.wait_ge(s["t_upd"], (LEVELS - 1) * iB + l)
                    if l > 1:
                        pe.wait_ge(s["x_ev"], (LEVELS - 1) * iB + l - 1)
                    for n in range(NCH):
                        ins = pe.matmul(chunk(b_x, n, HALF).rearrange("p (m h) -> p m h", h=h), chunk(LT[l], n),
                                        halves(chunk(T, n), h)[:, :, 0, :], start=True, stop=True)
                    ins.then_inc(s["x_mm"], 1)

                def t_products(l):
                    h = 1 << l
                    pe.wait_ge(s["x_ev"], (LEVELS - 1) * iB + l)
                    pe.wait_ge(s["tt_upd"], LEVELS * iB + l)
                    if l < LEVELS - 1:
                        for n in range(NCH):
                            pe.matmul(b_y[:, n * HALF:(n + 1) * HALF].rearrange("p (m h) -> p m h", h=h),
                                      chunk(TT[pB], n), halves(chunk(XS[l], n), h)[:, :, 0, :], start=True, stop=True)
                    for n in range(NCH):
                        ins = pe.matmul(b_y[:, 256 + n * HALF:256 + (n + 1) * HALF].rearrange("p (m h) -> p m h", h=h),
                                        chunk(XS[l], n), halves(chunk(TT[pB], n), h)[:, :, 1, :], start=True, stop=True)
                    ins.then_inc(s["y_mm"], 1)

                def state_update(n):
                    pe.wait_ge(s["w_ev"], NCH * iC + n + 1)
                    if n < 3:
                        if n == 0:
                            pe.wait_ge(s["kt_ev"], iC + 1)
                        pe.matmul(b_s[:, 2 * P:3 * P], chunk(kT[p], n), W[:, :], start=True, stop=True
                                  ).then_inc(s["su_mm"], 1)

                def chunk_outputs(n):
                    if n == 0:
                        after(pe, s["og_done"], iC)
                        pe.wait_ge(s["qk_ev"], LEVELS * (iC + 1))
                    else:
                        pe.matmul(chunk(b_o, n), kq[p][:, SEQ + n * P:SEQ + (n + 1) * P], S[(n - 1) % 2][:, :],
                                  start=True, stop=False)
                    pe.matmul(chunk(b_o, n), chunk(AT[p], n), W[:, :], start=n == 0, stop=True).then_inc(s["o_mm"], 1)

                def k_times_s(n):
                    pe.wait_ge(s["s_ready"], 3 * iC + n)
                    pe.matmul(b_s[:, 0:P], chunk(kq[p], n), S[(n - 1) % 2][:, :], start=True, stop=True
                              ).then_inc(s["ks_mm"], 1)

                def solve(n):
                    if n == 0:
                        pe.wait_ge(s["tt_upd"], LEVELS * (iC + 1))
                        pe.wait_ge(s["kq_ready"], (LEVELS + 1) * (iC + 1))
                        pe.wait_ge(s["vt_ev"], iC + 1)
                        after(pe, s["w_ev"], NCH * iC)
                    else:
                        pe.wait_ge(s["r_done"], 3 * iC + n)
                    pe.matmul(b_s[:, P:2 * P], chunk(TT[p], n), R[:, :] if n else chunk(vs[p], 0),
                              start=True, stop=True).then_inc(s["z_mm"], 1)

                for slot in range(8):
                    if C and 1 <= slot <= 4:
                        state_update(slot - 1)
                    if B and slot < LEVELS:
                        level(slot)
                    if B and slot >= 1:
                        lt_times_t(slot - 1)
                    if C and 1 <= slot <= 3:
                        k_times_s(slot)
                    if C and 1 <= slot <= 4:
                        chunk_outputs(slot - 1)
                    if C and slot == 0:
                        solve(0)
                    if slot == 0 and A:
                        pe.wait_ge(par_in[p], 16 * (j + 1))
                        pe.wait_ge(s["xt_ev"], KT * (bt + 1))
                        pe.wait_ge(s["ga_ev"], bt + 1)
                        after(pe, s["x2_add"], 2 * (i - 2))
                        project(0, "q_mm")
                    if slot == 1 and A:
                        pe.wait_ge(s["be_ev"], bt + 1)
                        project(1, "k_mm")
                    if slot == 2 and A:
                        pe.wait_ge(s["fa_ev"], bt + 1)
                        after(pe, s["raw_done"], i)
                        project(2, "v_mm")
                    if C and 1 <= slot <= 3:
                        solve(slot)
                    if slot == 2 and A:
                        pe.wait_ge(s["conv_done"], 3 * i + 1)
                        pe.matmul(b_q[:, :], par[p][:, FB:FB + P], faT[:, :], start=True, stop=True
                                  ).then_inc(s["f_mm"], 1)
                    if slot == 4 and B:
                        if A:
                            pe.wait_ge(s["conv_done"], 3 * i + 3)
                        else:
                            pe.wait_ge(s["raw_done"], i)
                        pe.wait_ge(s["silu_done"], 3 * (iB + 1))
                        for n in range(NCH):
                            ins = pe.transpose(chunk(b_v, n), chunk(v[pB], n), ident)
                        ins.then_inc(s["vt_mm"], 1)
                    if slot == 4 and A:
                        pe.wait_ge(s["conv_done"], 3 * i + 2)
                        for n in range(NCH):
                            ins = pe.matmul(chunk(b_k, n), chunk(gaT, n), par[p][:, GB:GB + P], start=True, stop=True)
                        ins.then_inc(s["g_mm"], 1)
                    if slot == 6 and C:
                        if A:
                            pe.wait_ge(s["sg_done"], i + 1)
                        pe.wait_ge(s["og_done"], iC + 1)
                        for n in range(NCH):
                            ins = pe.transpose(chunk(b_k, n), chunk(og, n), ident)
                        ins.then_inc(s["ogt_mm"], 1)
                    if slot == 7 and A:
                        if B:
                            pe.wait_ge(s["vt_ev"], iB + 1)
                        pe.wait_ge(s["conv_done"], 3 * i + 3)
                        pe.wait_ge(s["sq_done"], 2 * i + 2)
                        pe.wait_ge(s["qk_prod"], i + 1)
                        for t in range(3):
                            for n in range(NCH):
                                ins = pe.matmul(b_v[:, NCH * t + n:NCH * t + n + 1], chunk(y3[t], n), ones[:, 0:1],
                                                start=True, stop=True)
                        ins.then_inc(s["sums_mm"], 1)
                    if B and slot >= 2:
                        t_products(slot - 1)
                    if slot == 7 and B:
                        pe.wait_ge(s["kl_ready"], LEVELS * (iB + 1))
                        for n in range(3):
                            ins = pe.transpose(chunk(b_x, n), chunk(kl, n), ident)
                        ins.then_inc(s["kt_mm"], 1)
                    if slot == 7 and C:
                        if A:
                            pe.wait_ge(s["f_read"], i + 1)
                        pe.wait_ge(s["ogt_ev"], iC + 1)
                        for half in range(2):
                            for n in range(2):
                                ins = pe.matmul(bank[half][:, n * HID:(n + 1) * HID], chunk(ogT, 2 * half + n),
                                                wo_sb[:, bass.ds(hc * HID, HID)], start=True, stop=True)
                            ins.then_inc(s["out_mm"], 1)

            supersteps(pe, batch_stage, step)

            def ffn_block(m):
                pe.wait_ge(s["f_xn"], m + 1)
                turn_x("f_xT_mm")
                pe.wait_ge(s["f_xT_ev"], KT * (m + 1))
                after(pe, s["acc"], m * (EXPERTS + 1) * NCH)
                for n in range(NCH):
                    for t in range(KT):
                        ins = pe.matmul(b_v[:, n * EXPERTS:(n + 1) * EXPERTS],
                                        xT[:, t * SEQ + n * P:t * SEQ + (n + 1) * P], chunk(gw_sb, t, EXPERTS),
                                        start=t == 0, stop=t == KT - 1)
                ins.then_inc(s["r_mm"], 1)

                def up(e):
                    n = m * (EXPERTS + 1) + e
                    for part, done, free in ((0, "g2_mm", "silu2"), (1, "u2_mm", "h2")):
                        after(pe, s[free], n - 1)
                        for t in range(KT):
                            at = e * 3 * HID + part * HID + t * P
                            ins = pe.matmul(bank[3 + part + 2 * (e % 2)][:, :], lx[:, at:at + P], chunk(xT, t, SEQ),
                                            start=t == 0, stop=t == KT - 1)
                        ins.then_inc(s[done], 1)

                def down(e):
                    n = m * (EXPERTS + 1) + e
                    pe.wait_ge(s["h2"], n + 1)
                    if e == 0:
                        pe.wait_ge(s["r_sub"], m + 1)
                    for t in range(NCH):
                        if t % 2 == 0:
                            after(pe, s["acc"], NCH * n + t - 2)
                        ins = pe.matmul(bank[7 if t < 2 else 2][:, (t % 2) * HID:(t % 2 + 1) * HID],
                                        chunk(k[e % 2], t), lx[:, (3 * e + 2) * HID:(3 * e + 3) * HID],
                                        start=True, stop=True)
                        if t % 2:
                            ins.then_inc(s["d_mm"], 1)

                up(0)
                for e in range(EXPERTS + 1):
                    if e < EXPERTS:
                        up(e + 1)
                    down(e)

            pe.wait_ge(s["f_w"], 16)
            pe.wait_ge(s["x2_add"], 2 * NHEAD)
            pe.wait_ge(s["og_done"], NHEAD)
            ffn_block(0)
            with pe.Fori(1, BATCH) as m:
                ffn_block(m)


def kernel(**inputs):
    import numpy as np
    import concourse.bacc as bacc
    from concourse.bass_utils import run_bass_kernel_spmd

    A = {n.split("_", 2)[2]: np.asarray(v) for n, v in inputs.items()}

    def down_first(w):
        return w.reshape(w.shape[0], -1, P).transpose(2, 1, 0)

    qkv = np.stack([down_first(A[n]).reshape(P, KT, HEADS, P) for n in ("Wq", "Wk", "Wv")], 2)
    par = np.concatenate([
        qkv.transpose(3, 0, 1, 2, 4).reshape(HEADS, P, KT * 3 * P),
        A["Wfb"].reshape(HEADS, P, P).transpose(0, 2, 1),
        A["Wgb"].reshape(HEADS, P, P).transpose(0, 2, 1),
        *(A[n].reshape(HEADS, P, TAPS) for n in ("wq_conv", "wk_conv", "wv_conv")),
        A["dt_bias"].reshape(HEADS, P, 1),
        np.broadcast_to(A["A_log"].reshape(HEADS, 1, 1), (HEADS, P, 1))], 2)
    gates = np.concatenate([A["wg"], A["sg"][None]], 0)
    ups = np.concatenate([A["wu"], A["su"][None]], 0)
    downs = np.concatenate([A["wd"], A["sd"][None]], 0)
    ne = EXPERTS + 1
    ffn = np.stack([gates.reshape(ne, P, KT, P).transpose(3, 0, 2, 1).reshape(P, ne, HID),
                    ups.reshape(ne, P, KT, P).transpose(3, 0, 2, 1).reshape(P, ne, HID),
                    downs.transpose(2, 0, 1)], 2)
    arrays = {
        "x_dram": A["x"],
        "params_dram": par,
        "wfa_dram": down_first(A["Wfa"]).reshape(P, KT * P),
        "wga_dram": down_first(A["Wga"]).reshape(P, KT * P),
        "wb_dram": down_first(A["Wb"]).reshape(P, KT * HEADS),
        "wo_dram": A["Wo"].reshape(HID, HEADS, P).transpose(2, 1, 0).reshape(P, HEADS * HID),
        "onw_dram": A["o_norm_w"].reshape(P, 1),
        "gate_w_dram": down_first(A["gate_w"]).reshape(P, KT * EXPERTS),
        "ffn_dram": ffn.reshape(P, ne * 3 * HID),
    }
    arrays = {n: np.ascontiguousarray(v) for n, v in arrays.items()}
    nc = bacc.Bacc("TRN2", target_bir_lowering=False, num_devices=1)
    args = [nc.dram_tensor(n, v.shape, mybir.dt.from_np(v.dtype), kind="ExternalInput").ap()
            for n, v in arrays.items()]
    out = nc.dram_tensor("out_dram", (BATCH, SEQ, HID), F32, kind="ExternalOutput").ap()
    delta_moe(nc, *args, out)
    r = run_bass_kernel_spmd(nc, [arrays], core_ids=[0])
    return r.results[0]["out_dram"]
```

```python
from contextlib import ExitStack

import concourse.bass as bass
from concourse import mybir

ALU = mybir.AluOpType
ACT = mybir.ActivationFunctionType
F32 = mybir.dt.float32
U32 = mybir.dt.uint32
EXP_SET, LN_SET, SILU_SET = "exp_and_others", "natural_log", "silu_and_others"
AX_X = mybir.AxisListType.X

P = 128
BATCH, SEQ, HID = 16, 512, 256
HEADS, TAPS = 8, 4
EXPERTS = 8
KT = HID // P
NCH = SEQ // P
HALF = P // 2
LEVELS = 7
NHEAD = BATCH * HEADS
EPS_QK, EPS_NORM, EPS_LN = 1e-6, 1e-5, 1e-5

QKV = 0
FB = QKV + KT * 3 * P
GB = FB + P
CONV = GB + P
DT = CONV + 3 * TAPS
ALOG = DT + 1
PAR = ALOG + 1

TOT_AT = [None]
_at = 0
for _l in range(1, LEVELS + 1):
    TOT_AT.append(_at)
    _at += SEQ >> _l
TOT_LEN = _at



def halves(ap, h):
    return ap.rearrange("p (m two h) -> p m two h", two=2, h=h)


def after(eng, sem, value):
    if isinstance(value, int) and value <= 0:
        return
    eng.wait_ge(sem, value)


def delta_moe(nc, x, params, wfa, wga, wb, wo, onw, gate_w, ffn_w, out):
    with ExitStack() as ctx:
        def sb(name, shape, dt=F32):
            return ctx.enter_context(nc.sbuf_tensor(name, shape, dt))

        def sem(name):
            return ctx.enter_context(nc.semaphore(name))

        def chunk(t, n, w=P):
            return t[:, n * w:(n + 1) * w]

        bank = [ctx.enter_context(nc.psum_tensor(f"bank{n}", [P, 512], F32)) for n in range(8)]
        b_q, b_k, b_v, b_lvl, b_x, b_y, b_s, b_o = bank

        xall = sb("xall", [P, BATCH * NCH * HID])
        par = [sb(f"par{p}", [P, PAR]) for p in range(2)]
        wo_sb = sb("wo_sb", [P, HEADS * HID])
        onw_sb = sb("onw_sb", [P, 1])
        wfa_sb = sb("wfa_sb", [P, KT * P])
        wga_sb = sb("wga_sb", [P, KT * P])
        wb_sb = sb("wb_sb", [P, KT * HEADS])
        gw_sb = sb("gw_sb", [P, KT * EXPERTS])
        ident4 = sb("ident4", [P, SEQ])
        ident = ident4[:, 0:P]
        ones = sb("ones", [P, 1])
        plus_half = sb("plus_half", [P, NCH])
        minus_half = sb("minus_half", [P, NCH])
        mask = [sb(f"mask{l}", [P, NCH * HALF]) for l in range(LEVELS)]
        lower = sb("lower", [P, EXPERTS * EXPERTS])
        stats = sb("stats", [P, NCH * 6])
        mv = sb("mv", [P, NCH * 2])
        rstd = sb("rstd", [P, NCH])
        xn = sb("xn", [P, NCH * HID])
        xT = sb("xT", [P, KT * SEQ])
        faT = sb("faT", [P, SEQ])
        gaT = sb("gaT", [P, SEQ])
        bexp = sb("bexp", [P, NCH * HEADS])
        cw = [bexp, sb("cw1", [P, NCH * EXPERTS])]
        beta = sb("beta", [P, HEADS * NCH])
        y3 = [sb(f"y{n}", [P, SEQ]) for n in "qkv"]
        q = [sb(f"q{p}", [P, SEQ]) for p in range(2)]
        k = [sb(f"k{p}", [P, SEQ]) for p in range(2)]
        v = [sb(f"v{p}", [P, SEQ]) for p in range(2)]
        a = [sb(f"a{p}", [P, SEQ]) for p in range(2)]
        e_sb = sb("e_sb", [P, SEQ])
        w_sb = sb("w_sb", [P, SEQ])
        m_sb = sb("m_sb", [P, SEQ])
        amp = [sb(f"amp{p}", [P, 1]) for p in range(2)]
        xTs = [[chunk(xT, t, SEQ) for t in range(KT)], v]
        sg = [sb(f"sg{p}", [P, SEQ]) for p in range(2)]
        tk = [sb(f"tk{p}", [P, 8]) for p in range(2)]
        dg = [sb(f"dg{p}", [P, NCH]) for p in range(2)]
        rec = sb("rec", [P, NCH])
        sc = [sb(f"sc{p}", [P, NCH]) for p in range(2)]
        rinv = [sb(f"rinv{p}", [P, NCH]) for p in range(2)]
        eo = [sb(f"eo{p}", [P, NCH]) for p in range(2)]
        tot = [sb(f"tot{p}", [P, TOT_LEN]) for p in range(2)]
        kq = [sb(f"kq{p}", [P, 2 * SEQ]) for p in range(2)]
        kl = sb("kl", [P, SEQ])
        lx = sb("lx", [P, 2 * LEVELS * SEQ])
        LT = [lx[:, l * SEQ:(l + 1) * SEQ] for l in range(LEVELS)]
        XS = [lx[:, (LEVELS + l) * SEQ:(LEVELS + l + 1) * SEQ] for l in range(LEVELS)]
        T = sb("T", [P, SEQ])
        TT = [sb(f"TT{p}", [P, SEQ]) for p in range(2)]
        AT = [sb(f"AT{p}", [P, SEQ]) for p in range(2)]
        kT = [sb(f"kT{p}", [P, 3 * P]) for p in range(2)]
        vs = [sb(f"vs{p}", [P, SEQ]) for p in range(2)]
        R = sb("R", [P, P])
        W = sb("W", [P, P])
        S = [sb(f"S{p}", [P, P]) for p in range(2)]
        junk = sb("junk", [P, P])
        ss = sb("ss", [P, NCH])
        zz = sb("zz", [P, NCH])
        nrm = sb("nrm", [P, NCH])
        og = sb("og", [P, SEQ])
        ogT = sb("ogT", [P, SEQ])

        names = """pool_go dve_go sp_go x_in w_in consts halves_ok ident_ok zero_ok wo_ok par_in0 par_in1 amp_ok
        bn_st bn_mv bn_var bn_rs xn_ok xnT_mm xt_ev fa_mm ga_mm be_mm fa_ev ga_ev be_ev be_one beta_ok
        q_mm k_mm v_mm f_mm g_mm tap0 dtap conv_done silu_done sq_done qk_prod
        fabs e_done f_read w_done nr_done ln_done t1_done t2_done decay_done sg_done
        sums_mm tk_done raw_done rec_done sc_done rinv_done tot_step tot_done
        kq_ready kl_ready kcopy lvl_mm lt_done qk_ev at_init t_init tt_init t_upd tt_upd
        x_mm x_ev y_mm vt_mm vt_ev kt_mm kt_ev
        ks_mm r_done z_mm w_ev su_mm s_ready o_mm osq z_done nrm_done og_done
        ogt_mm ogt_ev out_mm x2_add
        mask_step f_w f_st f_mv f_var f_rs f_xn f_xT_mm f_xT_ev r_mm r_max r_sub r_exp r_sum r_rec r_sc
        r_gt r_eq r_eql r_any r_rank r_cw g2_mm u2_mm silu2 h2 d_mm acc stored""".split()
        s = {n: sem(n) for n in names}
        par_in = [s["par_in0"], s["par_in1"]]

        def tot_view(p, level):
            return a[p][:, :] if level == 0 else tot[p][:, TOT_AT[level]:TOT_AT[level] + (SEQ >> level)]

        block = ctx.enter_context(nc.Block())

        def supersteps(eng, batch_stage, step):
            def pair(j, bt, bc, ha, hc, A=True, B=(True, True), C=(True, True), nb=None):
                for p in range(2):
                    step(2 * j + p, j, p, bt, bc, ha + p, hc + p, A, B[p], C[p], nb)
            last, pairs = BATCH - 1, HEADS // 2
            batch_stage(0)
            pair(0, 0, 0, 0, 0, True, (False, True), (False, False))
            pair(1, 0, 0, 2, 0)
            with eng.Fori(2, pairs - 1) as hp:
                pair(hp, 0, 0, hp * 2, hp * 2 - 2)
            with eng.Fori(1, BATCH) as b:
                pair(b * pairs - 1, b - 1, b - 1, HEADS - 2, HEADS - 4, nb=b)
                batch_stage(b)
                pair(b * pairs, b, b - 1, 0, HEADS - 2)
                with eng.Fori(1, pairs - 1) as hp:
                    pair(b * pairs + hp, b, b, hp * 2, hp * 2 - 2)
            pair(NHEAD // 2 - 1, last, last, HEADS - 2, HEADS - 4)
            pair(NHEAD // 2, last, last, 0, HEADS - 2, False, (True, False), (True, True))

        def ffn_blocks(eng, prepare, ffn_block):
            prepare()
            for m in range(2):
                ffn_block(m, m, True)
            with eng.Fori(1, BATCH // 2 - 1) as mp:
                for p in range(2):
                    ffn_block(2 * mp + p, p, True)
            ffn_block(BATCH - 2, 0, True)
            ffn_block(BATCH - 1, 1, False)

        @block.sync
        def _(sp):
            for src, dst in ((wfa, wfa_sb), (wga, wga_sb), (wb, wb_sb), (wo, wo_sb), (onw, onw_sb), (gate_w, gw_sb)):
                sp.dma_start(dst[:, :], src).then_inc(s["w_in"], 16)
            xt = x.rearrange("b (n p) d -> p (b n) d", p=P)
            for b in range(BATCH):
                sp.dma_start(xall[:, b * NCH * HID:(b + 1) * NCH * HID].rearrange("p (n d) -> p n d", d=HID),
                             xt[:, b * NCH:(b + 1) * NCH, :]).then_inc(s["x_in"], 16)
                if b == 0:
                    for p in range(2):
                        sp.dma_start(par[p][:, :], params[p]).then_inc(par_in[p], 16)
                sp.wait_ge(s["x_in"], 16 * (b + 1))

            def load(i, p, h):
                for done, value in (("g_mm", i - 1), ("conv_done", 3 * (i - 1)), ("f_read", i - 1), ("decay_done", i - 1)):
                    sp.wait_ge(s[done], value)
                    sp.sem_inc(s["sp_go"], 1)
                sp.dma_start(par[p][:, :], params[h]).then_inc(par_in[p], 16)

            with sp.Fori(1, HEADS // 2) as hp:
                for p in range(2):
                    load(2 * hp + p, p, 2 * hp + p)
            with sp.Fori(1, BATCH) as b:
                with sp.Fori(0, HEADS // 2) as hp:
                    for p in range(2):
                        load(b * HEADS + 2 * hp + p, p, 2 * hp + p)
            sp.wait_ge(s["x_mm"], LEVELS * NHEAD)
            sp.wait_ge(s["y_mm"], (LEVELS - 1) * NHEAD)
            sp.wait_ge(s["x_ev"], (LEVELS - 1) * NHEAD)
            sp.wait_ge(s["tt_upd"], LEVELS * NHEAD)
            sp.dma_start(lx[:, 0:(EXPERTS + 1) * 3 * HID], ffn_w).then_inc(s["f_w"], 16)
            ot = out.rearrange("b (n p) d -> p (b n) d", p=P)
            with sp.Fori(0, BATCH) as m:
                sp.wait_ge(s["acc"], (m + 1) * (EXPERTS + 1) * NCH)
                sp.sem_inc(s["sp_go"], 1)
                sp.dma_start(ot[:, bass.ds(m * NCH, NCH), :],
                             xall[:, bass.ds(m * (NCH * HID), NCH * HID)].rearrange("p (n d) -> p n d", d=HID)
                             ).then_inc(s["stored"], 16)
            sp.wait_ge(s["stored"], 16 * BATCH)

        @block.gpsimd
        def _(pool):
            pool.memset(ident4[:, :], 0.0).then_inc(s["mask_step"], 1)
            pool.wait_ge(s["mask_step"], 1)
            pool.affine_select(out=ident4[:, :].rearrange("p (n c) -> p n c", c=P),
                               in_=ident4[:, :].rearrange("p (n c) -> p n c", c=P), compare_op=ALU.not_equal,
                               fill=1.0, base=0, pattern=[[0, NCH], [-1, P]], channel_multiplier=1
                               ).then_inc(s["ident_ok"], 1)
            pool.memset(ones[:, :], 1.0).then_inc(s["consts"], 1)
            pool.memset(plus_half[:, :], 0.5).then_inc(s["halves_ok"], 1)
            pool.memset(minus_half[:, :], -0.5).then_inc(s["halves_ok"], 1)
            pool.wait_ge(s["halves_ok"], 2)
            steps = 1
            for l in range(LEVELS):
                h, m = 1 << l, HALF >> l
                mv4 = mask[l][:, :].rearrange("p (n m h) -> p n m h", n=NCH, h=h)
                pool.memset(mask[l][:, :], 1.0).then_inc(s["mask_step"], 1)
                steps += 1
                pool.wait_ge(s["mask_step"], steps)
                pool.affine_select(out=mv4, in_=mv4, compare_op=ALU.is_ge, fill=0.0, base=0,
                                   pattern=[[0, NCH], [-2 * h, m], [0, h]], channel_multiplier=1
                                   ).then_inc(s["mask_step"], 1)
                steps += 1
                pool.wait_ge(s["mask_step"], steps)
                pool.affine_select(out=mv4, in_=mv4, compare_op=ALU.is_ge, fill=0.0, base=h - 1,
                                   pattern=[[0, NCH], [2 * h, m], [0, h]], channel_multiplier=-1
                                   ).then_inc(s["consts"], 1)
            pool.memset(lower[:, :], 1.0).then_inc(s["mask_step"], 1)
            pool.wait_ge(s["mask_step"], steps + 1)
            lo = lower[:, :].rearrange("p (e f) -> p e f", f=EXPERTS)
            pool.affine_select(out=lo, in_=lo, compare_op=ALU.is_gt, fill=0.0, base=0,
                               pattern=[[1, EXPERTS], [-1, EXPERTS]], channel_multiplier=0).then_inc(s["consts"], 1)

            def rstd_of(var, rs, m):
                pool.wait_ge(s[var], m + 1)
                pool.tensor_tensor(rstd[:, :], rstd[:, :], minus_half[:, :], ALU.pow).then_inc(s[rs], 1)

            def step(i, j, p, bt, bc, ha, hc, A, B, C, nb):
                iB, iC, pB = i - 1, i - 2, 1 - p

                def kl_update(l):
                    h = 1 << l
                    pool.wait_ge(s["lvl_mm"], LEVELS * iB + l + 1)
                    if l == 0:
                        after(pool, s["kt_mm"], iB)
                        src = halves(k[pB][:, :], h)[:, :, 0, :]
                        pool.wait_ge(s["silu_done"], 3 * iB + 2)
                    else:
                        pool.wait_ge(s["kl_ready"], LEVELS * iB + l)
                        if l == 1:
                            pool.wait_ge(s["kcopy"], iB + 1)
                        src = halves(kl[:, :], h)[:, :, 0, :]
                    totr = tot_view(pB, l).rearrange("p (m two) -> p m two", two=2)[:, :, 1:2]
                    pool.tensor_tensor(halves(kl[:, :], h)[:, :, 0, :], src,
                                       totr.broadcast_to([P, SEQ // (2 * h), h]), ALU.mult
                                       ).then_inc(s["kl_ready"], 1)

                if B:
                    pool.wait_ge(s["tot_done"], iB + 1)
                    kl_update(0)
                    after(pool, s["x_mm"], LEVELS * iB)
                    after(pool, s["t_upd"], (LEVELS - 1) * iB)
                    pool.sem_inc(s["pool_go"], 1)
                    pool.tensor_copy(T[:, :], ident4[:, :]).then_inc(s["t_init"], 1)
                    after(pool, s["z_mm"], NCH * (iB - 1))
                    pool.sem_inc(s["pool_go"], 1)
                    pool.tensor_copy(TT[pB][:, :], ident4[:, :]).then_inc(s["tt_init"], 1)
                    for l in range(1, 5):
                        kl_update(l)
                if A:
                    pool.wait_ge(s["ln_done"], i + 1)
                    pool.tensor_tensor(e_sb[:, :], e_sb[:, :], w_sb[:, :], ALU.subtract).then_inc(s["t1_done"], 1)
                    pool.wait_ge(s["t1_done"], i + 1)
                    pool.wait_ge(s["f_read"], i + 1)
                    pool.tensor_tensor(e_sb[:, :], e_sb[:, :], m_sb[:, :], ALU.subtract).then_inc(s["t2_done"], 1)
                if C:
                    pool.wait_ge(s["z_done"], iC + 1)
                    after(pool, s["og_done"], iC)
                    pool.tensor_tensor(nrm[:, :], zz[:, :], minus_half[:, :], ALU.pow).then_inc(s["nrm_done"], 1)
                if B:
                    kl_update(5)
                if A:
                    pool.wait_ge(s["decay_done"], i + 1)
                    after(pool, s["s_ready"], 3 * (i - 1))
                    for l in range(1, LEVELS + 1):
                        if l > 1:
                            pool.wait_ge(s["tot_step"], (LEVELS - 1) * i + l - 1)
                        two = tot_view(p, l - 1).rearrange("p (m two) -> p m two", two=2)
                        pool.tensor_tensor(tot_view(p, l).unsqueeze(2), two[:, :, 0:1], two[:, :, 1:2], ALU.mult
                                           ).then_inc(s["tot_step" if l < LEVELS else "tot_done"], 1)
                    pool.wait_ge(s["silu_done"], 3 * i + 3)
                    pool.tensor_tensor(y3[2][:, :], q[p][:, :], k[p][:, :], ALU.mult).then_inc(s["qk_prod"], 1)
                if B:
                    kl_update(6)
                if A:
                    pool.wait_ge(s["tk_done"], i + 1)
                    after(pool, s["vt_ev"], i - 1)
                    pool.tensor_tensor(rinv[p][:, :], tk[p][:, 4:8], plus_half[:, :], ALU.pow).then_inc(s["rinv_done"], 1)

                if nb is not None and p == 0:
                    rstd_of("bn_var", "bn_rs", nb)

            rstd_of("bn_var", "bn_rs", 0)
            supersteps(pool, lambda bn: None, step)
            rstd_of("f_var", "f_rs", 0)
            with pool.Fori(1, BATCH) as m:
                rstd_of("f_var", "f_rs", m)

        @block.scalar
        def _(act):
            act.preload_act_table_set(EXP_SET)

            def batch_stage(bn):
                for t in range(KT):
                    act.wait_ge(s["xnT_mm"], KT * bn + t + 1)
                    act.activation(chunk(xT, t, SEQ), (b_lvl, b_y)[t][:, :], ACT.Copy).then_inc(s["xt_ev"], 1)
                act.wait_ge(s["be_mm"], bn + 1)
                after(act, s["beta_ok"], bn)
                act.activation(bexp[:, :], b_s[:, 0:NCH * HEADS], ACT.Exp, scale=-1.0).then_inc(s["be_ev"], 1)
                act.wait_ge(s["fa_mm"], bn + 1)
                act.activation(faT[:, :], b_v[:, :], ACT.Copy).then_inc(s["fa_ev"], 1)
                act.wait_ge(s["ga_mm"], bn + 1)
                act.activation(gaT[:, :], b_x[:, :], ACT.Copy).then_inc(s["ga_ev"], 1)

            def step(i, j, p, bt, bc, ha, hc, A, B, C, nb):
                iB, iC, pB = i - 1, i - 2, 1 - p

                def tap0(t, mm):
                    act.wait_ge(s[mm], i + 1)
                    if t == 0:
                        act.wait_ge(par_in[p], 16 * (j + 1))
                        after(act, s["sums_mm"], i)
                    at = CONV + t * TAPS + TAPS - 1
                    act.activation(y3[t][:, :], bank[t][:, :], ACT.Copy, scale=par[p][:, at:at + 1]
                                   ).then_inc(s["tap0"], 1)

                def x_evict(l):
                    h = 1 << l
                    act.wait_ge(s["x_mm"], LEVELS * iB + l + 1)
                    after(act, s["y_mm"], (LEVELS - 1) * iB - (LEVELS - 1) + l)
                    if l == 1:
                        act.wait_ge(s["zero_ok"], 1)
                    act.activation(halves(XS[l], h)[:, :, 0, :],
                                   halves(b_x[:, :], h)[:, :, 0, :], ACT.Copy
                                   ).then_inc(s["x_ev"], 1)

                def w_evict(n):
                    act.wait_ge(s["z_mm"], NCH * iC + n + 1)
                    act.wait_ge(s["sc_done"], iC + 1)
                    act.activation(W[:, :], b_s[:, P:2 * P], ACT.Copy, scale=sc[p][:, n:n + 1]).then_inc(s["w_ev"], 1)

                def turned_v():
                    act.wait_ge(s["vt_mm"], iB + 1)
                    act.wait_ge(s["rinv_done"], iB + 1)
                    after(act, s["o_mm"], NCH * (iB - 1))
                    for n in range(NCH):
                        ins = act.activation(chunk(vs[pB], n), chunk(b_v, n), ACT.Copy, scale=rinv[pB][:, n:n + 1])
                    ins.then_inc(s["vt_ev"], 1)

                for slot in range(8):
                    if slot == 0 and B:
                        after(act, s["kt_mm"], iB)
                        act.activation(halves(kl[:, :], 1)[:, :, 1, :], halves(k[pB][:, :], 1)[:, :, 1, :], ACT.Copy
                                       ).then_inc(s["kcopy"], 1)
                    if slot == 0 and C:
                        w_evict(0)
                    if slot == 3 and A:
                        act.wait_ge(s["f_mm"], i + 1)
                        after(act, s["t2_done"], i)
                        act.activation(e_sb[:, :], b_q[:, :], ACT.Abs, bias=par[p][:, DT:DT + 1]).then_inc(s["fabs"], 1)
                        act.wait_ge(s["fabs"], i + 1)
                        act.activation(e_sb[:, :], e_sb[:, :], ACT.Exp, scale=-1.0).then_inc(s["e_done"], 1)
                        act.activation(amp[p][:, :], par[p][:, ALOG:ALOG + 1], ACT.Exp).then_inc(s["amp_ok"], 1)
                        act.preload_act_table_set(LN_SET)
                    if slot == 5 and A:
                        if B:
                            x_evict(4)
                        act.wait_ge(s["t2_done"], i + 1)
                        act.wait_ge(s["amp_ok"], i + 1)
                        after(act, s["tot_done"], i - 1)
                        act.activation(a[p][:, :], e_sb[:, :], ACT.Exp, scale=amp[p][:, 0:1]
                                       ).then_inc(s["decay_done"], 1)
                    if slot == 5 and A:
                        act.preload_act_table_set(SILU_SET)
                        after(act, s["lvl_mm"], LEVELS * (i - 1))
                        after(act, s["kl_ready"], LEVELS * (i - 1))
                        after(act, s["vt_mm"], i - 1)
                        for t, dst in enumerate((q, k, v)):
                            act.wait_ge(s["conv_done"], 3 * i + t + 1)
                            act.activation(dst[p][:, :], y3[t][:, :], ACT.Silu).then_inc(s["silu_done"], 1)
                    if slot == 7 and C:
                        act.wait_ge(s["ogt_mm"], iC + 1)
                        after(act, s["out_mm"], 2 * iC)
                        act.activation(ogT[:, :], b_k[:, :], ACT.Copy).then_inc(s["ogt_ev"], 1)
                    if B and slot >= 2 and not (A and slot in (5, 6)):
                        x_evict(slot - 1)
                    if 1 <= slot <= 3 and C:
                        w_evict(slot)
                    if slot < 3 and A:
                        tap0(slot, ("q_mm", "k_mm", "v_mm")[slot])
                    if slot == 4:
                        if A:
                            act.wait_ge(s["nr_done"], i + 1)
                            act.activation(w_sb[:, :], w_sb[:, :], ACT.Ln).then_inc(s["ln_done"], 1)
                            act.preload_act_table_set(EXP_SET)
                        if C:
                            act.wait_ge(s["o_mm"], NCH * (iC + 1))
                            after(act, s["z_done"], iC)
                            for n in range(NCH):
                                if n:
                                    act.wait_ge(s["osq"], NCH * iC + n)
                                act.activation(junk[:, :], chunk(b_o, n), ACT.Square, accum_out=ss[:, n:n + 1]
                                               ).then_inc(s["osq"], 1)
                    if slot == 6:
                        if B:
                            if A:
                                x_evict(5)
                            turned_v()
                        if A:
                            act.wait_ge(s["g_mm"], i + 1)
                            after(act, s["og_done"], i - 1)
                            act.activation(sg[p][:, :], b_k[:, :], ACT.Sigmoid).then_inc(s["sg_done"], 1)
                    if slot == 6 and A:
                        for t, src in enumerate((q, k)):
                            act.wait_ge(s["silu_done"], 3 * i + t + 1)
                            act.activation(y3[t][:, :], src[p][:, :], ACT.Square).then_inc(s["sq_done"], 1)
                    if slot == 7:
                        if B:
                            act.wait_ge(s["kt_mm"], iB + 1)
                            act.activation(kT[pB][:, :], b_x[:, 0:3 * P], ACT.Copy).then_inc(s["kt_ev"], 1)
                        if A:
                            act.preload_act_table_set(EXP_SET)

            supersteps(act, batch_stage, step)

            def evict_x(m, p):
                for t in range(KT):
                    act.wait_ge(s["f_xT_mm"], KT * m + t + 1)
                    act.activation(xTs[p][t][:, :], bank[t][:, :], ACT.Copy).then_inc(s["f_xT_ev"], 1)

            def exponentials(m, p):
                act.wait_ge(s["r_sub"], m + 1)
                act.activation(cw[p][:, :], cw[p][:, :], ACT.Exp).then_inc(s["r_exp"], 1)
                act.preload_act_table_set(SILU_SET)

            def prepare():
                evict_x(0, 0)
                exponentials(0, 0)

            def ffn_block(m, p, more):
                for e in range(EXPERTS + 1):
                    n = m * (EXPERTS + 1) + e
                    act.wait_ge(s["g2_mm"], n + 1)
                    after(act, s["h2"], n - 1)
                    act.activation(q[e % 2][:, :], bank[3 + 2 * (e % 2)][:, :], ACT.Silu).then_inc(s["silu2"], 1)
                    if more and e == 5:
                        evict_x(m + 1, 1 - p)
                if more:
                    exponentials(m + 1, 1 - p)

            ffn_blocks(act, prepare, ffn_block)

        @block.vector
        def _(dve):
            dve.memset(lx[:, :], 0.0).then_inc(s["zero_ok"], 1)
            dve.wait_ge(s["w_in"], 16 * 6)
            dve.tensor_scalar(wo_sb[:, :], wo_sb[:, :], onw_sb[:, 0:1], None, ALU.mult).then_inc(s["wo_ok"], 1)
            dve.wait_ge(s["consts"], 2 + LEVELS)
            dve.wait_ge(s["ident_ok"], 1)
            dve.wait_ge(s["zero_ok"], 1)

            def ln_moments(m, st, mvs, var):
                for n in range(NCH):
                    ins = dve.bn_stats(chunk(stats, n, 6), xall[:, bass.ds(m * (NCH * HID) + n * HID, HID)])
                ins.then_inc(s[st], 1)
                dve.wait_ge(s[st], m + 1)
                dve.sem_inc(s["dve_go"], 1)
                for n in range(NCH):
                    ins = dve.bn_aggr(chunk(mv, n, 2), chunk(stats, n, 6))
                ins.then_inc(s[mvs], 1)
                dve.wait_ge(s[mvs], m + 1)
                dve.tensor_scalar(rstd[:, :].unsqueeze(2),
                                  mv[:, :].rearrange("p (n two) -> p n two", two=2)[:, :, 1:2],
                                  EPS_LN, None, ALU.add).then_inc(s[var], 1)

            def ln_scale(m, rs, done, turned):
                dve.wait_ge(s[rs], m + 1)
                after(dve, s[turned], KT * m)
                for n in range(NCH):
                    ins = dve.tensor_scalar(chunk(xn, n, HID), xall[:, bass.ds(m * (NCH * HID) + n * HID, HID)],
                                            mv[:, 2 * n:2 * n + 1], rstd[:, n:n + 1], ALU.subtract, ALU.mult)
                ins.then_inc(s[done], 1)

            def batch_stage(bn):
                dve.wait_ge(s["be_ev"], bn + 1)
                dve.tensor_scalar(bexp[:, :], bexp[:, :], 1.0, None, ALU.add).then_inc(s["be_one"], 1)
                dve.wait_ge(s["be_one"], bn + 1)
                dve.reciprocal(beta[:, :].rearrange("p (h n) -> p n h", n=NCH),
                               bexp[:, :].rearrange("p (n h) -> p n h", h=HEADS)).then_inc(s["beta_ok"], 1)

            def step(i, j, p, bt, bc, ha, hc, A, B, C, nb):
                iB, iC, pB = i - 1, i - 2, 1 - p

                def l_evict(l):
                    h = 1 << l
                    dve.wait_ge(s["lvl_mm"], LEVELS * iB + l + 1)
                    if l == 0:
                        dve.wait_ge(s["sc_done"], iB + 1)
                    after(dve, s["x_mm"], LEVELS * iB - LEVELS + l + 1)
                    for n in range(NCH):
                        ins = dve.scalar_tensor_tensor(
                            out=halves(chunk(LT[l], n), h)[:, :, 1, :],
                            in0=b_lvl[:, n * HALF:(n + 1) * HALF].rearrange("p (m h) -> p m h", h=h),
                            scalar=sc[pB][:, n:n + 1],
                            in1=mask[l][:, 0:HALF].rearrange("p (m h) -> p m h", h=h), op0=ALU.mult, op1=ALU.mult)
                    ins.then_inc(s["lt_done"], 1)

                def kq_update(l):
                    h = 1 << l
                    m = SEQ // (2 * h)
                    dve.wait_ge(s["kq_ready"], (LEVELS + 1) * iB + l + 1)
                    if l == 0:
                        dve.wait_ge(s["tot_done"], iB + 1)
                    totl = tot_view(pB, l).rearrange("p (m two) -> p m two", two=2)[:, :, 0:1]
                    for part in range(2):
                        view = halves(chunk(kq[pB], part, SEQ), h)[:, :, 1, :]
                        ins = dve.tensor_tensor(view, view, totl.broadcast_to([P, m, h]), ALU.mult)
                    ins.then_inc(s["kq_ready"], 1)

                def qk_evict(l):
                    h = 1 << l
                    if l == 0:
                        dve.wait_ge(s["at_init"], iB + 1)
                    else:
                        dve.wait_ge(s["qk_ev"], LEVELS * iB + l)
                    dve.sem_inc(s["dve_go"], 1)
                    dve.copy_predicated(halves(AT[pB][:, :], h)[:, :, 1, :],
                                        mask[l][:, :].bitcast(U32).rearrange("p (m h) -> p m h", h=h),
                                        b_lvl[:, 256:512].rearrange("p (m h) -> p m h", h=h)).then_inc(s["qk_ev"], 1)

                def t_update(l):
                    h = 1 << l
                    tl = halves(T[:, :], h)[:, :, 0, :]
                    tr = halves(TT[pB][:, :], h)[:, :, 1, :]
                    if l == 0:
                        dve.wait_ge(s["t_init"], iB + 1)
                        dve.wait_ge(s["tt_init"], iB + 1)
                        dve.wait_ge(s["x_mm"], LEVELS * iB + 1)
                        dve.wait_ge(s["lt_done"], LEVELS * iB + 1)
                        dve.tensor_tensor(tl, tl, halves(b_x[:, :], h)[:, :, 0, :],
                                          ALU.subtract).then_inc(s["t_upd"], 1)
                        dve.tensor_tensor(tr, tr, halves(LT[0], h)[:, :, 1, :], ALU.subtract).then_inc(s["tt_upd"], 1)
                        return
                    dve.wait_ge(s["y_mm"], (LEVELS - 1) * iB + l)
                    if l < LEVELS - 1:
                        dve.wait_ge(s["t_upd"], (LEVELS - 1) * iB + l)
                        dve.tensor_tensor(tl, tl, b_y[:, 0:256].rearrange("p (m h) -> p m h", h=h),
                                          ALU.subtract).then_inc(s["t_upd"], 1)
                    dve.wait_ge(s["tt_upd"], LEVELS * iB + l)
                    dve.tensor_tensor(tr, tr, b_y[:, 256:512].rearrange("p (m h) -> p m h", h=h),
                                      ALU.subtract).then_inc(s["tt_upd"], 1)

                def conv(t):
                    dve.wait_ge(s["tap0"], 3 * i + t + 1)
                    for d in range(1, TAPS):
                        at = CONV + t * TAPS + TAPS - 1 - d
                        if d > 1:
                            dve.wait_ge(s["dtap"], 2 * (3 * i + t) + d - 1)
                        ins = dve.scalar_tensor_tensor(out=y3[t][:, d:SEQ], in0=bank[t][:, 0:SEQ - d],
                                                       scalar=par[p][:, at:at + 1], in1=y3[t][:, d:SEQ],
                                                       op0=ALU.mult, op1=ALU.add)
                        ins.then_inc(s["dtap" if d < TAPS - 1 else "conv_done"], 1)

                def s_update(n):
                    dve.wait_ge(s["su_mm"], 3 * iC + n + 1)
                    su = b_s[:, 2 * P:3 * P]
                    if n == 0:
                        dve.tensor_copy(S[0][:, :], su).then_inc(s["s_ready"], 1)
                        return
                    if n == 1:
                        dve.wait_ge(s["tot_done"], iC + 1)
                    dve.wait_ge(s["s_ready"], 3 * iC + n)
                    dve.scalar_tensor_tensor(out=S[n % 2][:, :], in0=S[(n - 1) % 2][:, :],
                                             scalar=tot_view(p, LEVELS)[:, n:n + 1], in1=su,
                                             op0=ALU.mult, op1=ALU.add).then_inc(s["s_ready"], 1)

                def residual(n):
                    dve.wait_ge(s["ks_mm"], 3 * iC + n)
                    dve.wait_ge(s["vt_ev"], iC + 1)
                    dve.tensor_tensor(R[:, :], chunk(vs[p], n), b_s[:, 0:P], ALU.subtract).then_inc(s["r_done"], 1)

                def outputs():
                    dve.wait_ge(s["nrm_done"], iC + 1)
                    dve.wait_ge(s["sg_done"], iC + 1)
                    after(dve, s["ogt_mm"], iC)
                    for n in range(NCH):
                        ins = dve.scalar_tensor_tensor(out=chunk(og, n), in0=chunk(b_o, n),
                                                       scalar=nrm[:, n:n + 1], in1=chunk(sg[p], n),
                                                       op0=ALU.mult, op1=ALU.mult)
                    ins.then_inc(s["og_done"], 1)

                for slot in range(8):
                    if C and 1 <= slot <= 3:
                        s_update(slot - 1)
                    if B and slot < LEVELS:
                        l_evict(slot)
                    if C and 1 <= slot <= 3:
                        residual(slot)
                    if B and slot < LEVELS:
                        kq_update(slot)
                        qk_evict(slot)
                    if B and slot == 1:
                        t_update(0)
                    if A and 1 <= slot <= 3:
                        conv(slot - 1)
                    if C and slot == 5:
                        outputs()
                    if A and slot == 7:
                        dve.wait_ge(s["sums_mm"], i + 1)
                        after(dve, s["rinv_done"], i - 1)
                        dve.tensor_scalar(tk[p][:, :], b_v[:, 0:8], P * EPS_QK, None, ALU.add).then_inc(s["tk_done"], 1)
                        dve.tensor_copy(dg[p][:, :], b_v[:, 8:12]).then_inc(s["raw_done"], 1)
                        dve.wait_ge(s["tk_done"], i + 1)
                        dve.reciprocal(rec[:, :], tk[p][:, 4:8]).then_inc(s["rec_done"], 1)
                        dve.tensor_scalar(eo[p][:, :], tk[p][:, 0:4], P * EPS_NORM, None, ALU.mult)
                        dve.wait_ge(s["rec_done"], i + 1)
                        dve.wait_ge(s["beta_ok"], bt + 1)
                        after(dve, s["w_ev"], NCH * (i - 1))
                        dve.tensor_tensor(sc[p][:, :], rec[:, :], beta[:, bass.ds(ha * NCH, NCH)], ALU.mult
                                          ).then_inc(s["sc_done"], 1)
                    if nb is not None and slot == 6:
                        if p == 0:
                            dve.wait_ge(s["x_in"], nb * 16 + 16)
                            ln_moments(nb, "bn_st", "bn_mv", "bn_var")
                        else:
                            ln_scale(nb, "bn_rs", "xn_ok", "xnT_mm")
                    if B and slot >= 2:
                        t_update(slot - 1)
                    if A and slot == 3:
                        dve.wait_ge(s["fabs"], i + 1)
                        after(dve, s["t2_done"], i)
                        dve.tensor_scalar(m_sb[:, :], b_q[:, :], par[p][:, DT:DT + 1], 0.0, ALU.add, ALU.max
                                          ).then_inc(s["f_read"], 1)
                        dve.wait_ge(s["e_done"], i + 1)
                        dve.tensor_scalar(w_sb[:, :], e_sb[:, :], 1.0, None, ALU.add).then_inc(s["w_done"], 1)
                        dve.wait_ge(s["w_done"], i + 1)
                        dve.scalar_tensor_tensor(out=e_sb[:, :], in0=w_sb[:, :], scalar=1.0, in1=e_sb[:, :],
                                                 op0=ALU.subtract, op1=ALU.subtract).then_inc(s["nr_done"], 1)
                    if C and slot == 4:
                        dve.wait_ge(s["osq"], NCH * (iC + 1))
                        after(dve, s["nrm_done"], iC)
                        dve.scalar_tensor_tensor(out=zz[:, :], in0=ss[:, :], scalar=1.0 / P, in1=eo[p][:, :],
                                                 op0=ALU.mult, op1=ALU.add).then_inc(s["z_done"], 1)
                    if A and slot == 6:
                        dve.wait_ge(s["decay_done"], i + 1)
                        after(dve, s["o_mm"], NCH * (i - 1))
                        dve.wait_ge(s["silu_done"], 3 * i + 2)
                        dve.tensor_tensor(chunk(kq[p], 1, SEQ), q[p][:, :], a[p][:, :], ALU.mult)
                        dve.tensor_tensor(chunk(kq[p], 0, SEQ), k[p][:, :], a[p][:, :], ALU.mult
                                          ).then_inc(s["kq_ready"], 1)
                    if A and slot == 7:
                        dve.wait_ge(s["raw_done"], i + 1)
                        for n in range(NCH):
                            ins = dve.tensor_scalar(chunk(AT[p], n), ident, dg[p][:, n:n + 1], None, ALU.mult)
                        ins.then_inc(s["at_init"], 1)
                    if C and slot == 7:
                        for half in range(2):
                            dve.wait_ge(s["out_mm"], 2 * iC + half + 1)
                            after(dve, s["x2_add"], 2 * iC + half)
                            at = bass.ds(bc * (NCH * HID) + half * 512, 512)
                            dve.tensor_tensor(xall[:, at], xall[:, at], bank[half][:, :], ALU.add
                                              ).then_inc(s["x2_add"], 1)

            dve.wait_ge(s["x_in"], 16)
            ln_moments(0, "bn_st", "bn_mv", "bn_var")
            ln_scale(0, "bn_rs", "xn_ok", "xnT_mm")
            supersteps(dve, batch_stage, step)

            E8 = [P, NCH, EXPERTS]

            def logits(m, p):
                lg = bank[0][:, 0:NCH * EXPERTS].rearrange("p (n e) -> p n e", e=EXPERTS)
                ex = cw[p][:, :].rearrange("p (n e) -> p n e", e=EXPERTS)
                dve.wait_ge(s["r_mm"], m + 1)
                dve.tensor_reduce(rec[:, :], lg, AX_X, ALU.max).then_inc(s["r_max"], 1)
                dve.wait_ge(s["r_max"], m + 1)
                dve.tensor_tensor(ex, lg, rec[:, :].unsqueeze(2).broadcast_to(E8), ALU.subtract).then_inc(s["r_sub"], 1)

            def router(m, p):
                ex = cw[p][:, :].rearrange("p (n e) -> p n e", e=EXPERTS)
                score = beta[:, :].rearrange("p (n e) -> p n e", e=EXPERTS)
                gt = e_sb[:, 0:256].rearrange("p (n e f) -> p n e f", n=NCH, e=EXPERTS)
                eq = w_sb[:, 0:256].rearrange("p (n e f) -> p n e f", n=NCH, e=EXPERTS)
                e84 = [P, NCH, EXPERTS, EXPERTS]
                dve.wait_ge(s["r_exp"], m + 1)
                dve.tensor_reduce(zz[:, :], ex, AX_X, ALU.add).then_inc(s["r_sum"], 1)
                dve.wait_ge(s["r_sum"], m + 1)
                dve.reciprocal(ss[:, :], zz[:, :]).then_inc(s["r_rec"], 1)
                dve.wait_ge(s["r_rec"], m + 1)
                dve.tensor_tensor(score, ex, ss[:, :].unsqueeze(2).broadcast_to(E8), ALU.mult).then_inc(s["r_sc"], 1)
                dve.wait_ge(s["r_sc"], m + 1)
                other = score.unsqueeze(2).broadcast_to(e84)
                own = score.unsqueeze(3).broadcast_to(e84)
                dve.tensor_tensor(gt, other, own, ALU.is_gt).then_inc(s["r_gt"], 1)
                dve.tensor_tensor(eq, other, own, ALU.is_equal).then_inc(s["r_eq"], 1)
                dve.wait_ge(s["r_eq"], m + 1)
                lows = lower[:, :].rearrange("p (e f) -> p e f", f=EXPERTS).unsqueeze(1).broadcast_to(e84)
                dve.tensor_tensor(eq, eq, lows, ALU.mult).then_inc(s["r_eql"], 1)
                dve.wait_ge(s["r_eql"], m + 1)
                dve.wait_ge(s["r_gt"], m + 1)
                dve.tensor_tensor(gt, gt, eq, ALU.add).then_inc(s["r_any"], 1)
                dve.wait_ge(s["r_any"], m + 1)
                dve.tensor_reduce(ex, gt, AX_X, ALU.add).then_inc(s["r_rank"], 1)
                dve.wait_ge(s["r_rank"], m + 1)
                dve.scalar_tensor_tensor(out=ex, in0=ex, scalar=1.5, in1=score, op0=ALU.is_lt, op1=ALU.mult
                                         ).then_inc(s["r_cw"], 1)
                dve.wait_ge(s["r_cw"], m + 1)

            def ffn_block(m, p, more):
                def hidden(e):
                    n = m * (EXPERTS + 1) + e
                    dve.wait_ge(s["silu2"], n + 1)
                    dve.wait_ge(s["u2_mm"], n + 1)
                    after(dve, s["d_mm"], 2 * (n - 1))
                    dve.tensor_tensor(k[e % 2][:, :], q[e % 2][:, :], bank[4 + 2 * (e % 2)][:, :], ALU.mult
                                      ).then_inc(s["h2"], 1)

                def add(e):
                    n = m * (EXPERTS + 1) + e
                    for t in range(NCH):
                        if t % 2 == 0:
                            dve.wait_ge(s["d_mm"], 2 * n + t // 2 + 1)
                        after(dve, s["acc"], NCH * n + t - NCH + 1)
                        at = bass.ds(m * (NCH * HID) + t * HID, HID)
                        dve.scalar_tensor_tensor(
                            out=xall[:, at], in0=bank[7 if t < 2 else 2][:, (t % 2) * HID:(t % 2 + 1) * HID],
                            scalar=1.0 if e == EXPERTS else cw[p][:, t * EXPERTS + e:t * EXPERTS + e + 1],
                            in1=xall[:, at], op0=ALU.mult, op1=ALU.add).then_inc(s["acc"], 1)

                hidden(0)
                router(m, p)
                for e in range(EXPERTS + 1):
                    if e < EXPERTS:
                        hidden(e + 1)
                    if more and e == 2:
                        ln_moments(m + 1, "f_st", "f_mv", "f_var")
                    if more and e == 4:
                        ln_scale(m + 1, "f_rs", "f_xn", "f_xT_mm")
                    if more and e == EXPERTS:
                        logits(m + 1, 1 - p)
                    add(e)

            def prepare():
                ln_moments(0, "f_st", "f_mv", "f_var")
                ln_scale(0, "f_rs", "f_xn", "f_xT_mm")
                logits(0, 0)

            dve.wait_ge(s["x2_add"], 2 * NHEAD)
            ffn_blocks(dve, prepare, ffn_block)

        @block.tensor
        def _(pe):
            pe.wait_ge(s["ident_ok"], 1)
            pe.wait_ge(s["consts"], 1)
            pe.wait_ge(s["w_in"], 16 * 6)
            pe.wait_ge(s["zero_ok"], 1)
            pe.wait_ge(s["wo_ok"], 1)

            def turn_x(dst, dst_sem):
                for t in range(KT):
                    for n in range(NCH):
                        ins = pe.transpose(chunk(dst[t], n), xn[:, n * HID + t * P:n * HID + (t + 1) * P], ident)
                    ins.then_inc(s[dst_sem], 1)

            def batch_stage(bn):
                pe.wait_ge(s["xn_ok"], bn + 1)
                after(pe, s["qk_ev"], LEVELS * (HEADS * bn - 1))
                after(pe, s["tt_upd"], LEVELS * (HEADS * bn - 1))
                turn_x((b_lvl, b_y), "xnT_mm")
                pe.wait_ge(s["xt_ev"], KT * (bn + 1))
                after(pe, s["w_ev"], NCH * (HEADS * bn - 2))
                for n in range(NCH):
                    for t in range(KT):
                        ins = pe.matmul(b_s[:, n * HEADS:(n + 1) * HEADS], xT[:, t * SEQ + n * P:t * SEQ + (n + 1) * P],
                                        chunk(wb_sb, t, HEADS), start=t == 0, stop=t == KT - 1)
                ins.then_inc(s["be_mm"], 1)
                after(pe, s["raw_done"], HEADS * bn)
                after(pe, s["kt_ev"], HEADS * bn - 1)
                for w, dst, done in ((wfa_sb, b_v, "fa_mm"), (wga_sb, b_x, "ga_mm")):
                    for t in range(KT):
                        ins = pe.matmul(dst[:, :], chunk(w, t), chunk(xT, t, SEQ), start=t == 0, stop=t == KT - 1)
                    ins.then_inc(s[done], 1)

            def step(i, j, p, bt, bc, ha, hc, A, B, C, nb):
                iB, iC, pB = i - 1, i - 2, 1 - p

                def project(t, done, between=None):
                    for kt in range(KT):
                        if kt == 1 and between:
                            between()
                        at = QKV + (kt * 3 + t) * P
                        ins = pe.matmul(bank[t][:, :], par[p][:, at:at + P], chunk(xT, kt, SEQ),
                                        start=kt == 0, stop=kt == KT - 1)
                    ins.then_inc(s[done], 1)

                def level(l):
                    h = 1 << l
                    pe.wait_ge(s["kq_ready"], (LEVELS + 1) * iB + l + 1)
                    if l:
                        pe.wait_ge(s["kl_ready"], LEVELS * iB + l)
                    if l == 1:
                        pe.wait_ge(s["kcopy"], iB + 1)
                    after(pe, s["qk_ev"], LEVELS * iB + l)
                    left = kl if l else k[pB]
                    right = kq[pB][:, :].rearrange("p (q n m two h) -> p q n m two h", q=2, n=NCH, two=2, h=h)
                    dst = b_lvl[:, :].rearrange("p (q n m h) -> p q n m h", q=2, n=NCH, h=h)
                    for n in range(NCH):
                        ins = pe.matmul(dst[:, :, n], chunk(left, n), right[:, :, n, :, 1, :], start=True, stop=True)
                    ins.then_inc(s["lvl_mm"], 1)

                def lt_times_t(l):
                    pe.wait_ge(s["lt_done"], LEVELS * iB + l + 1)
                    if l == 0:
                        after(pe, s["kt_ev"], iB)
                        for n in range(NCH):
                            ins = pe.transpose(chunk(b_x, n), chunk(LT[0], n), ident)
                        ins.then_inc(s["x_mm"], 1)
                        return
                    pe.wait_ge(s["t_upd"], (LEVELS - 1) * iB + l)
                    if l > 1:
                        pe.wait_ge(s["x_ev"], (LEVELS - 1) * iB + l - 1)
                    for n in range(NCH):
                        ins = pe.matmul(chunk(b_x, n), chunk(LT[l], n), chunk(T, n), start=True, stop=True)
                    ins.then_inc(s["x_mm"], 1)

                def t_products(l):
                    h = 1 << l
                    pe.wait_ge(s["x_ev"], (LEVELS - 1) * iB + l)
                    pe.wait_ge(s["tt_upd"], LEVELS * iB + l)
                    if l < LEVELS - 1:
                        for n in range(NCH):
                            pe.matmul(b_y[:, n * HALF:(n + 1) * HALF].rearrange("p (m h) -> p m h", h=h),
                                      chunk(TT[pB], n), halves(chunk(XS[l], n), h)[:, :, 0, :], start=True, stop=True)
                    for n in range(NCH):
                        ins = pe.matmul(b_y[:, 256 + n * HALF:256 + (n + 1) * HALF].rearrange("p (m h) -> p m h", h=h),
                                        chunk(XS[l], n), halves(chunk(TT[pB], n), h)[:, :, 1, :], start=True, stop=True)
                    ins.then_inc(s["y_mm"], 1)

                def state_update(n):
                    pe.wait_ge(s["w_ev"], NCH * iC + n + 1)
                    if n < 3:
                        if n == 0:
                            pe.wait_ge(s["kt_ev"], iC + 1)
                        pe.matmul(b_s[:, 2 * P:3 * P], chunk(kT[p], n), W[:, :], start=True, stop=True
                                  ).then_inc(s["su_mm"], 1)

                def chunk_outputs(n):
                    if n == 0:
                        after(pe, s["og_done"], iC)
                        pe.wait_ge(s["qk_ev"], LEVELS * (iC + 1))
                    else:
                        pe.matmul(chunk(b_o, n), kq[p][:, SEQ + n * P:SEQ + (n + 1) * P], S[(n - 1) % 2][:, :],
                                  start=True, stop=False)
                    pe.matmul(chunk(b_o, n), chunk(AT[p], n), W[:, :], start=n == 0, stop=True).then_inc(s["o_mm"], 1)

                def k_times_s(n):
                    pe.wait_ge(s["s_ready"], 3 * iC + n)
                    pe.matmul(b_s[:, 0:P], chunk(kq[p], n), S[(n - 1) % 2][:, :], start=True, stop=True
                              ).then_inc(s["ks_mm"], 1)

                def solve(n):
                    if n == 0:
                        pe.wait_ge(s["be_ev"], bt + 1)
                        pe.wait_ge(s["tt_upd"], LEVELS * (iC + 1))
                        pe.wait_ge(s["kq_ready"], (LEVELS + 1) * (iC + 1))
                        pe.wait_ge(s["vt_ev"], iC + 1)
                        after(pe, s["w_ev"], NCH * iC)
                    else:
                        pe.wait_ge(s["r_done"], 3 * iC + n)
                    pe.matmul(b_s[:, P:2 * P], chunk(TT[p], n), R[:, :] if n else chunk(vs[p], 0),
                              start=True, stop=True).then_inc(s["z_mm"], 1)

                for slot in range(8):
                    if C and 1 <= slot <= 4:
                        state_update(slot - 1)
                    if B and slot < LEVELS:
                        level(slot)
                    if C and slot == 4:
                        chunk_outputs(3)
                    if B and slot >= 1:
                        lt_times_t(slot - 1)
                    if slot == 7 and C:
                        if A:
                            pe.wait_ge(s["sg_done"], i + 1)
                        pe.wait_ge(s["og_done"], iC + 1)
                        for n in range(NCH):
                            ins = pe.transpose(chunk(b_k, n), chunk(og, n), ident)
                        ins.then_inc(s["ogt_mm"], 1)
                    if C and 1 <= slot <= 3:
                        k_times_s(slot)
                        chunk_outputs(slot - 1)
                    if C and slot == 0:
                        solve(0)
                    if slot == 0 and A:
                        pe.wait_ge(par_in[p], 16 * (j + 1))
                        pe.wait_ge(s["xt_ev"], KT * (bt + 1))
                        pe.wait_ge(s["ga_ev"], bt + 1)
                        after(pe, s["x2_add"], 2 * (i - 2))
                        project(0, "q_mm")
                    if slot == 1 and A:
                        project(1, "k_mm", (lambda: solve(1)) if C else None)
                    if slot == 2 and A:
                        pe.wait_ge(s["fa_ev"], bt + 1)
                        after(pe, s["raw_done"], i)
                        project(2, "v_mm", (lambda: solve(2)) if C else None)
                    if C and (slot == 3 or slot in (1, 2) and not A):
                        solve(slot)
                    if slot == 2 and A:
                        pe.wait_ge(s["conv_done"], 3 * i + 1)
                        pe.matmul(b_q[:, :], par[p][:, FB:FB + P], faT[:, :], start=True, stop=True
                                  ).then_inc(s["f_mm"], 1)
                    if slot in (3, 4, 5) and A:
                        if slot == 3:
                            pe.wait_ge(s["conv_done"], 3 * i + 2)
                        for n in {3: (0,), 4: (1, 2), 5: (3,)}[slot]:
                            ins = pe.matmul(chunk(b_k, n), chunk(gaT, n), par[p][:, GB:GB + P], start=True, stop=True)
                        if slot == 5:
                            ins.then_inc(s["g_mm"], 1)
                    if slot == 6 and B:
                        if A:
                            pe.wait_ge(s["conv_done"], 3 * i + 3)
                        else:
                            pe.wait_ge(s["raw_done"], i)
                        pe.wait_ge(s["silu_done"], 3 * (iB + 1))
                        for n in range(NCH):
                            ins = pe.transpose(chunk(b_v, n), chunk(v[pB], n), ident)
                        ins.then_inc(s["vt_mm"], 1)
                    if slot == 7 and A:
                        if B:
                            pe.wait_ge(s["vt_ev"], iB + 1)
                        pe.wait_ge(s["conv_done"], 3 * i + 3)
                        pe.wait_ge(s["sq_done"], 2 * i + 2)
                        pe.wait_ge(s["qk_prod"], i + 1)
                        for t in range(3):
                            for n in range(NCH):
                                ins = pe.matmul(b_v[:, NCH * t + n:NCH * t + n + 1], chunk(y3[t], n), ones[:, 0:1],
                                                start=True, stop=True)
                        ins.then_inc(s["sums_mm"], 1)
                    if B and slot >= 2:
                        t_products(slot - 1)
                    if slot == 7 and B:
                        pe.wait_ge(s["kl_ready"], LEVELS * (iB + 1))
                        for n in range(3):
                            ins = pe.transpose(chunk(b_x, n), chunk(kl, n), ident)
                        ins.then_inc(s["kt_mm"], 1)
                    if slot == 7 and C:
                        if A:
                            pe.wait_ge(s["f_read"], i + 1)
                        pe.wait_ge(s["ogt_ev"], iC + 1)
                        for half in range(2):
                            for n in range(2):
                                ins = pe.matmul(bank[half][:, n * HID:(n + 1) * HID], chunk(ogT, 2 * half + n),
                                                wo_sb[:, bass.ds(hc * HID, HID)], start=True, stop=True)
                            ins.then_inc(s["out_mm"], 1)

            supersteps(pe, batch_stage, step)

            def turn_next(m):
                pe.wait_ge(s["f_xn"], m + 1)
                after(pe, s["r_sub"], m)
                turn_x(bank, "f_xT_mm")

            def route(m, p):
                pe.wait_ge(s["f_xT_ev"], KT * (m + 1))
                for n in range(NCH):
                    for t in range(KT):
                        ins = pe.matmul(bank[0][:, n * EXPERTS:(n + 1) * EXPERTS], chunk(xTs[p][t], n),
                                        chunk(gw_sb, t, EXPERTS), start=t == 0, stop=t == KT - 1)
                ins.then_inc(s["r_mm"], 1)

            def ffn_block(m, p, more):
                def up(e):
                    n = m * (EXPERTS + 1) + e
                    for part, done, free in ((0, "g2_mm", "silu2"), (1, "u2_mm", "h2")):
                        after(pe, s[free], n - 1)
                        for t in range(KT):
                            at = e * 3 * HID + part * HID + t * P
                            ins = pe.matmul(bank[3 + part + 2 * (e % 2)][:, :], lx[:, at:at + P], xTs[p][t][:, :],
                                            start=t == 0, stop=t == KT - 1)
                        ins.then_inc(s[done], 1)

                def down(e):
                    n = m * (EXPERTS + 1) + e
                    pe.wait_ge(s["h2"], n + 1)
                    for t in range(NCH):
                        if t % 2 == 0:
                            after(pe, s["acc"], NCH * n + t - 2)
                        ins = pe.matmul(bank[7 if t < 2 else 2][:, (t % 2) * HID:(t % 2 + 1) * HID],
                                        chunk(k[e % 2], t), lx[:, (3 * e + 2) * HID:(3 * e + 3) * HID],
                                        start=True, stop=True)
                        if t % 2:
                            ins.then_inc(s["d_mm"], 1)

                up(0)
                for e in range(EXPERTS + 1):
                    if e < EXPERTS:
                        up(e + 1)
                    if more and e == EXPERTS - 1:
                        route(m + 1, 1 - p)
                    down(e)
                    if more and e == 4:
                        turn_next(m + 1)

            def prepare():
                turn_next(0)
                route(0, 0)

            pe.wait_ge(s["f_w"], 16)
            pe.wait_ge(s["x2_add"], 2 * NHEAD)
            pe.wait_ge(s["og_done"], NHEAD)
            ffn_blocks(pe, prepare, ffn_block)


def kernel(**inputs):
    import numpy as np
    import concourse.bacc as bacc
    from concourse.bass_utils import run_bass_kernel_spmd

    A = {n.split("_", 2)[2]: np.asarray(v) for n, v in inputs.items()}

    def down_first(w):
        return w.reshape(w.shape[0], -1, P).transpose(2, 1, 0)

    qkv = np.stack([down_first(A[n]).reshape(P, KT, HEADS, P) for n in ("Wq", "Wk", "Wv")], 2)
    par = np.concatenate([
        qkv.transpose(3, 0, 1, 2, 4).reshape(HEADS, P, KT * 3 * P),
        A["Wfb"].reshape(HEADS, P, P).transpose(0, 2, 1),
        A["Wgb"].reshape(HEADS, P, P).transpose(0, 2, 1),
        *(A[n].reshape(HEADS, P, TAPS) for n in ("wq_conv", "wk_conv", "wv_conv")),
        A["dt_bias"].reshape(HEADS, P, 1),
        np.broadcast_to(A["A_log"].reshape(HEADS, 1, 1), (HEADS, P, 1))], 2)
    gates = np.concatenate([A["wg"], A["sg"][None]], 0)
    ups = np.concatenate([A["wu"], A["su"][None]], 0)
    downs = np.concatenate([A["wd"], A["sd"][None]], 0)
    ne = EXPERTS + 1
    ffn = np.stack([gates.reshape(ne, P, KT, P).transpose(3, 0, 2, 1).reshape(P, ne, HID),
                    ups.reshape(ne, P, KT, P).transpose(3, 0, 2, 1).reshape(P, ne, HID),
                    downs.transpose(2, 0, 1)], 2)
    arrays = {
        "x_dram": A["x"],
        "params_dram": par,
        "wfa_dram": down_first(A["Wfa"]).reshape(P, KT * P),
        "wga_dram": down_first(A["Wga"]).reshape(P, KT * P),
        "wb_dram": down_first(A["Wb"]).reshape(P, KT * HEADS),
        "wo_dram": A["Wo"].reshape(HID, HEADS, P).transpose(2, 1, 0).reshape(P, HEADS * HID),
        "onw_dram": A["o_norm_w"].reshape(P, 1),
        "gate_w_dram": down_first(A["gate_w"]).reshape(P, KT * EXPERTS),
        "ffn_dram": ffn.reshape(P, ne * 3 * HID),
    }
    arrays = {n: np.ascontiguousarray(v) for n, v in arrays.items()}
    nc = bacc.Bacc("TRN2", target_bir_lowering=False, num_devices=1)
    args = [nc.dram_tensor(n, v.shape, mybir.dt.from_np(v.dtype), kind="ExternalInput").ap()
            for n, v in arrays.items()]
    out = nc.dram_tensor("out_dram", (BATCH, SEQ, HID), F32, kind="ExternalOutput").ap()
    delta_moe(nc, *args, out)
    r = run_bass_kernel_spmd(nc, [arrays], core_ids=[0])
    return r.results[0]["out_dram"]
```
